# Optimizing a Trainium2 kernel written in Bass

```python
import numpy as np
import jax
import jax.numpy as jnp

def _softmax(x, axis=-1):
    return jax.nn.softmax(x, axis=axis)

def _gelu(x):
    return jax.nn.gelu(x, approximate=True)

def _silu(x):
    return jax.nn.silu(x)

def _sigmoid(x):
    return jax.nn.sigmoid(x)

def _layernorm(x, axis=-1, eps=1e-05):
    m = jnp.mean(x, axis=axis, keepdims=True)
    v = jnp.var(x, axis=axis, keepdims=True)
    return (x - m) / jnp.sqrt(v + eps)

def _scatter_add(tgt, idx, src, axis=0):
    return tgt.at[idx].add(src)

def _segment_sum(src, seg, n):
    return jax.ops.segment_sum(src, seg, n)
kernel_name = 'mk_adaln_ffn_d2_seqx_r8_9db5fb'

def setup_inputs(seed: int=0):
    np.random.seed(seed)
    _w = jnp.asarray

    def _rec_inputs():
        import jax
        import jax.numpy as jnp
        _rk = jax.random.key(seed)
        x = 7.22e-05 + 1 * jax.random.normal(jax.random.fold_in(_rk, 1), (32, 32, 512), jnp.float32)
        _lenS = 32 - jax.random.randint(jax.random.fold_in(_rk, 7), (32,), 0, max(1, 32 // 4) + 1, jnp.int32)
        _lenS2 = 32 - jax.random.randint(jax.random.fold_in(_rk, 8), (32,), 0, max(1, 32 // 4) + 1, jnp.int32)
        itok_B_2_6 = jax.random.randint(jax.random.fold_in(_rk, 11), (32,), 2, 7, jnp.int32)
        itok_B_0_7 = jax.random.randint(jax.random.fold_in(_rk, 12), (32,), 0, 8, jnp.int32)
        return (x, itok_B_2_6, itok_B_0_7)
    x, itok_B_2_6, itok_B_0_7 = _rec_inputs()

    def _L0_cond_setup():
        import jax, jax.numpy as jnp
        import numpy as np
        B, N, H, F = (4, 64, 512, 1376)
        L, R, RANK = (1, 16, 16)
        SCALE = 0.5
        key = jax.random.key(seed)
        ks = jax.random.split(key, 12)
        nrm = lambda k, shape, fan: jax.random.normal(k, shape, jnp.float32) * fan ** (-0.5)
        inp = {'x': jax.random.normal(ks[0], (B, N, H), jnp.float32), 'W_gate': nrm(ks[1], (F, H), H), 'W_up': nrm(ks[2], (F, H), H), 'W_down': nrm(ks[3], (H, F), F), 'A_gate': nrm(ks[4], (L, R, RANK, H), H), 'B_gate': nrm(ks[5], (L, R, F, RANK), RANK), 'A_up': nrm(ks[6], (L, R, RANK, H), H), 'B_up': nrm(ks[7], (L, R, F, RANK), RANK), 'A_down': nrm(ks[8], (L, R, RANK, F), F), 'B_down': nrm(ks[9], (L, R, H, RANK), RANK), 'lora_indices': jax.random.randint(ks[10], (B,), 0, R), 'layer_idx': 0}
        return inp
    _L0_cond_all = _L0_cond_setup()
    _L0_cond_in = {k: v for k, v in _L0_cond_all.items() if k in ('W_gate', 'W_up', 'W_down', 'A_gate', 'B_gate', 'A_up', 'B_up', 'A_down', 'B_down')}
    del _L0_cond_all

    def _L0_ffn_setup():
        import jax, jax.numpy as jnp
        import numpy as np
        IN, OUT = (512, 512)
        R_TOP, R_INT = (64, 4)
        R_TAIL = min(IN, OUT) - R_TOP
        B, S = (4, 128)
        key = jax.random.key(seed)
        ks = jax.random.split(key, 10)
        sc = 1.0 / np.sqrt(OUT)
        x = jax.random.normal(ks[0], (B, S, IN), jnp.float32)
        U_top = jax.random.normal(ks[1], (OUT, R_TOP), jnp.float32) * sc
        Vh_top = jax.random.normal(ks[2], (R_TOP, IN), jnp.float32) * sc
        U_tail = jax.random.normal(ks[3], (OUT, R_TAIL), jnp.float32) * sc
        Vh_tail = jax.random.normal(ks[4], (R_TAIL, IN), jnp.float32) * sc
        S_top = jnp.sort(jax.random.uniform(ks[5], (R_TOP,), jnp.float32, 1.0, 10.0))[::-1]
        S_tail = jnp.sort(jax.random.uniform(ks[6], (R_TAIL,), jnp.float32, 0.01, 1.0))[::-1]
        U_tail_r = U_tail[:, :R_INT]
        S_tail_r = S_tail[:R_INT]
        Vh_tail_r = Vh_tail[:R_INT, :]
        alpha = jnp.ones((R_TOP,), jnp.float32)
        beta = jnp.zeros((R_TOP,), jnp.float32)
        D = jnp.ones((R_INT,), jnp.float32)
        R = jnp.eye(R_INT, dtype=jnp.float32) + 0.01 * jax.random.normal(ks[7], (R_INT, R_INT), jnp.float32)
        bias = jax.random.normal(ks[8], (OUT,), jnp.float32) * 0.02
        return dict(x=x, U_top=U_top, S_top=S_top, Vh_top=Vh_top, U_tail=U_tail, S_tail=S_tail, Vh_tail=Vh_tail, U_tail_r=U_tail_r, S_tail_r=S_tail_r, Vh_tail_r=Vh_tail_r, alpha=alpha, beta=beta, D=D, R=R, bias=bias)
    _L0_ffn_all = _L0_ffn_setup()
    _L0_ffn_in = {k: v for k, v in _L0_ffn_all.items() if k in ('U_top', 'S_top', 'Vh_top', 'U_tail', 'S_tail', 'Vh_tail', 'U_tail_r', 'S_tail_r', 'Vh_tail_r', 'alpha', 'beta', 'D', 'R', 'bias')}
    del _L0_ffn_all

    def _L1_cond_setup():
        import jax, jax.numpy as jnp
        import numpy as np
        TOP_K = 2
        LANG_BIAS = 5.0
        SCALING = 32.0 / 16.0
        LANGUAGE_PAD_ID = -1
        key = jax.random.key(seed)
        ks = jax.random.split(key, 6)
        B, T, D, O, E, R = (4, 256, 512, 512, 8, 16)
        x = jax.random.normal(ks[0], (B, T, D), dtype=jnp.float32)
        language_ids = jax.random.randint(ks[1], (B,), 0, E).astype(jnp.int64)
        W = jax.random.normal(ks[2], (O, D), dtype=jnp.float32) * (1.0 / np.sqrt(D))
        Wr = jax.random.normal(ks[3], (E, D), dtype=jnp.float32) * (1.0 / np.sqrt(D))
        A = jax.random.normal(ks[4], (E, R, D), dtype=jnp.float32) * (1.0 / np.sqrt(D))
        Bm = jax.random.normal(ks[5], (O, R), dtype=jnp.float32) * 0.0
        Bm = jnp.broadcast_to(Bm, (E, O, R)) + jax.random.normal(ks[5], (E, O, R), dtype=jnp.float32) * 0.02
        return {'x': x, 'language_ids': language_ids, 'W': W, 'Wr': Wr, 'A': A, 'B': Bm}
    _L1_cond_all = _L1_cond_setup()
    _L1_cond_in = {k: v for k, v in _L1_cond_all.items() if k in ('W', 'Wr', 'A', 'B')}
    del _L1_cond_all

    def _L1_ffn_setup():
        import jax, jax.numpy as jnp
        import numpy as np
        EPS = 1e-06
        QMAX = 127.0

        def _quant_act(x):
            s = jnp.max(jnp.abs(x), axis=-1, keepdims=True) / QMAX
            s = jnp.maximum(s, 1e-08)
            q = jnp.clip(jnp.round(x / s), -QMAX, QMAX)
            return (q, s)

        def _quant_w(W):
            ws = jnp.max(jnp.abs(W), axis=1, keepdims=True) / QMAX
            ws = jnp.maximum(ws, 1e-08)
            Wq = jnp.clip(jnp.round(W / ws), -QMAX, QMAX)
            return (Wq, ws)
        key = jax.random.key(seed)
        k1, k2, k3, k4, k5 = jax.random.split(key, 5)
        B, S, D, I = (4, 256, 512, 1376)
        return {'hidden_states': jax.random.normal(k1, (B, S, D), dtype=jnp.float32), 'rmsnorm_weight': jax.random.uniform(k2, (D,), dtype=jnp.float32), 'Wg': jax.random.normal(k3, (I, D), dtype=jnp.float32) * 0.02, 'Wu': jax.random.normal(k4, (I, D), dtype=jnp.float32) * 0.02, 'Wd': jax.random.normal(k5, (D, I), dtype=jnp.float32) * 0.02}
    _L1_ffn_all = _L1_ffn_setup()
    _L1_ffn_in = {k: v for k, v in _L1_ffn_all.items() if k in ('rmsnorm_weight', 'Wg', 'Wu', 'Wd')}
    del _L1_ffn_all
    return {'x': x, 'itok_B_2_6': itok_B_2_6, 'itok_B_0_7': itok_B_0_7, 'L0_cond_W_gate': _L0_cond_in['W_gate'], 'L0_cond_W_up': _L0_cond_in['W_up'], 'L0_cond_W_down': _L0_cond_in['W_down'], 'L0_cond_A_gate': _L0_cond_in['A_gate'], 'L0_cond_B_gate': _L0_cond_in['B_gate'], 'L0_cond_A_up': _L0_cond_in['A_up'], 'L0_cond_B_up': _L0_cond_in['B_up'], 'L0_cond_A_down': _L0_cond_in['A_down'], 'L0_cond_B_down': _L0_cond_in['B_down'], 'L0_ffn_U_top': _L0_ffn_in['U_top'], 'L0_ffn_S_top': _L0_ffn_in['S_top'], 'L0_ffn_Vh_top': _L0_ffn_in['Vh_top'], 'L0_ffn_U_tail': _L0_ffn_in['U_tail'], 'L0_ffn_S_tail': _L0_ffn_in['S_tail'], 'L0_ffn_Vh_tail': _L0_ffn_in['Vh_tail'], 'L0_ffn_U_tail_r': _L0_ffn_in['U_tail_r'], 'L0_ffn_S_tail_r': _L0_ffn_in['S_tail_r'], 'L0_ffn_Vh_tail_r': _L0_ffn_in['Vh_tail_r'], 'L0_ffn_alpha': _L0_ffn_in['alpha'], 'L0_ffn_beta': _L0_ffn_in['beta'], 'L0_ffn_D': _L0_ffn_in['D'], 'L0_ffn_R': _L0_ffn_in['R'], 'L0_ffn_bias': _L0_ffn_in['bias'], 'L1_cond_W': _L1_cond_in['W'], 'L1_cond_Wr': _L1_cond_in['Wr'], 'L1_cond_A': _L1_cond_in['A'], 'L1_cond_B': _L1_cond_in['B'], 'L1_ffn_rmsnorm_weight': _L1_ffn_in['rmsnorm_weight'], 'L1_ffn_Wg': _L1_ffn_in['Wg'], 'L1_ffn_Wu': _L1_ffn_in['Wu'], 'L1_ffn_Wd': _L1_ffn_in['Wd']}

def reference(x, itok_B_2_6, itok_B_0_7, L0_cond_W_gate, L0_cond_W_up, L0_cond_W_down, L0_cond_A_gate, L0_cond_B_gate, L0_cond_A_up, L0_cond_B_up, L0_cond_A_down, L0_cond_B_down, L0_ffn_U_top, L0_ffn_S_top, L0_ffn_Vh_top, L0_ffn_U_tail, L0_ffn_S_tail, L0_ffn_Vh_tail, L0_ffn_U_tail_r, L0_ffn_S_tail_r, L0_ffn_Vh_tail_r, L0_ffn_alpha, L0_ffn_beta, L0_ffn_D, L0_ffn_R, L0_ffn_bias, L1_cond_W, L1_cond_Wr, L1_cond_A, L1_cond_B, L1_ffn_rmsnorm_weight, L1_ffn_Wg, L1_ffn_Wu, L1_ffn_Wd):
    import jax
    import jax.numpy as jnp

    def _L0_cond_ref(x, W_gate, W_up, W_down, A_gate, B_gate, A_up, B_up, A_down, B_down, lora_indices, layer_idx):
        import jax, jax.numpy as jnp
        import numpy as np
        B, N, H, F = (4, 64, 512, 1376)
        L, R, RANK = (1, 16, 16)
        SCALE = 0.5

        def lora_add(base, inp, A, B):
            Ab = A[layer_idx][lora_indices]
            Bb = B[layer_idx][lora_indices]
            t = jnp.einsum('bri,bni->bnr', Ab, inp)
            return base + jnp.einsum('bor,bnr->bno', Bb, t) * SCALE
        gate = lora_add(jnp.einsum('bnh,fh->bnf', x, W_gate), x, A_gate, B_gate)
        up = lora_add(jnp.einsum('bnh,fh->bnf', x, W_up), x, A_up, B_up)
        act = jax.nn.silu(gate) * up
        down = lora_add(jnp.einsum('bnf,hf->bnh', act, W_down), act, A_down, B_down)
        return down

    def _L0_ffn_ref(x, U_top, S_top, Vh_top, U_tail, S_tail, Vh_tail, U_tail_r, S_tail_r, Vh_tail_r, alpha, beta, D, R, bias):
        import jax, jax.numpy as jnp
        import numpy as np
        IN, OUT = (512, 512)
        R_TOP, R_INT = (64, 4)
        R_TAIL = min(IN, OUT) - R_TOP
        B, S = (4, 128)
        s_head = jax.nn.relu(S_top * alpha + beta)
        W_head = U_top * s_head[None, :] @ Vh_top
        W_tail = U_tail * S_tail[None, :] @ Vh_tail
        Bm = U_tail_r * S_tail_r[None, :]
        delta = Bm * jax.nn.relu(D)[None, :] @ R @ Vh_tail_r
        W_eff = W_head + W_tail + delta
        return jnp.einsum('bsi,oi->bso', x, W_eff) + bias

    def _L1_cond_ref(x, language_ids, W, Wr, A, B):
        import jax, jax.numpy as jnp
        import numpy as np
        TOP_K = 2
        LANG_BIAS = 5.0
        SCALING = 32.0 / 16.0
        LANGUAGE_PAD_ID = -1
        base = jnp.einsum('btd,od->bto', x, W)
        E = Wr.shape[0]
        logits = jnp.einsum('btd,ed->bte', x.astype(jnp.float32), Wr.astype(jnp.float32))
        expert_targets = language_ids
        valid = expert_targets >= 0
        tgt = jnp.where(valid, expert_targets, 0)
        bias = jax.nn.one_hot(tgt, E, dtype=logits.dtype) * LANG_BIAS
        bias = jnp.where(valid[:, None], bias, 0.0)
        logits = logits + bias[:, None, :]
        topw, topi = jax.lax.top_k(logits, TOP_K)
        weights = jax.nn.softmax(topw, axis=-1)
        gates = jnp.sum(jax.nn.one_hot(topi, E, dtype=weights.dtype) * weights[..., None], axis=-2)
        gates = gates.astype(x.dtype)
        h = jnp.einsum('btd,erd->bter', x, A)
        lora_out = jnp.einsum('bter,bte,eor->bto', h, gates, B)
        return base + SCALING * lora_out

    def _L1_ffn_ref(hidden_states, rmsnorm_weight, Wg, Wu, Wd):
        import jax, jax.numpy as jnp
        import numpy as np
        EPS = 1e-06
        QMAX = 127.0

        def _quant_act(x):
            s = jnp.max(jnp.abs(x), axis=-1, keepdims=True) / QMAX
            s = jnp.maximum(s, 1e-08)
            q = jnp.clip(jnp.round(x / s), -QMAX, QMAX)
            return (q, s)

        def _quant_w(W):
            ws = jnp.max(jnp.abs(W), axis=1, keepdims=True) / QMAX
            ws = jnp.maximum(ws, 1e-08)
            Wq = jnp.clip(jnp.round(W / ws), -QMAX, QMAX)
            return (Wq, ws)
        B, S, D = hidden_states.shape
        x = hidden_states.reshape(B * S, D)
        x = x * jax.lax.rsqrt(jnp.mean(x * x, axis=-1, keepdims=True) + EPS)
        x = x * rmsnorm_weight
        q, s = _quant_act(x)
        Wgq, wsg = _quant_w(Wg)
        Wuq, wsu = _quant_w(Wu)
        gate = jnp.einsum('td,id->ti', q, Wgq) * s * wsg.T
        up = jnp.einsum('td,id->ti', q, Wuq) * s * wsu.T
        h = jax.nn.silu(gate) * up
        q2, s2 = _quant_act(h)
        Wdq, wsd = _quant_w(Wd)
        out = jnp.einsum('ti,di->td', q2, Wdq) * s2 * wsd.T
        return out.reshape(B, S, D)
    x = x + _L0_ffn_ref(_L0_cond_ref(x, L0_cond_W_gate, L0_cond_W_up, L0_cond_W_down, L0_cond_A_gate, L0_cond_B_gate, L0_cond_A_up, L0_cond_B_up, L0_cond_A_down, L0_cond_B_down, itok_B_2_6, 0), L0_ffn_U_top, L0_ffn_S_top, L0_ffn_Vh_top, L0_ffn_U_tail, L0_ffn_S_tail, L0_ffn_Vh_tail, L0_ffn_U_tail_r, L0_ffn_S_tail_r, L0_ffn_Vh_tail_r, L0_ffn_alpha, L0_ffn_beta, L0_ffn_D, L0_ffn_R, L0_ffn_bias)
    x = x + _L1_ffn_ref(_L1_cond_ref(x, itok_B_0_7, L1_cond_W, L1_cond_Wr, L1_cond_A, L1_cond_B), L1_ffn_rmsnorm_weight, L1_ffn_Wg, L1_ffn_Wu, L1_ffn_Wd)
    return x

_drawn_inputs = setup_inputs


def setup_inputs(seed=0):
    import zlib

    import numpy as np

    out = dict(_drawn_inputs(seed))
    spreads = {'L0_ffn_alpha': (1.0, 0.2), 'L0_ffn_beta': (0.0, 0.571), 'L0_ffn_D': (1.0, 0.6)}
    factors = {'L0_ffn_S_tail_r': 26.115,
     'L0_ffn_bias': 8.0,
     'L1_cond_W': 7.143,
     'L1_cond_Wr': 8.0,
     'L1_cond_A': 8.0,
     'L1_cond_B': 8.0,
     'L1_ffn_rmsnorm_weight': 8.0,
     'L1_ffn_Wg': 7.143,
     'L1_ffn_Wu': 7.072,
     'L1_ffn_Wd': 7.094}
    for name, (base, spread) in spreads.items():
        noise = np.random.default_rng([zlib.crc32(name.encode()), seed]).standard_normal(out[name].shape)
        drawn = base * np.exp(spread * noise) if base else spread * noise
        out[name] = jnp.asarray(drawn.astype(out[name].dtype))
    for name, factor in factors.items():
        out[name] = (out[name] * factor).astype(out[name].dtype)
    return out
```

```python
import concourse.bass as bass
from concourse import mybir
from contextlib import ExitStack

P = 128
T = 1024
H = 512
F = 1376
FT = 11
FP = FT * P
FREM = F - (FT - 1) * P
KT = H // P
NB = 512
NH = T // NB
BATCH, SEQ = 32, 32
EXPERTS, RANK = 16, 16
GB = P // RANK
GT = GB * SEQ
HB = BATCH // NH
E8, R8 = 8, 16
TILES = T // P
HT = E8 * R8 + E8
LORA_SCALE = 0.5
MOE_SCALE = 2.0
LANG_BIAS = 5.0
RMS_EPS = 1e-6
QMAX = 127.0
Q_GUARD = 1e-8
ROUND = 12582912.0
CH = (459, 459, 458)
CO = (0, 459, 918)
WCH = KT
STEPS = NH * FT
C_FIRST = 17 + 4 * FT
CONSTS = C_FIRST + GT + 2 * P + TILES * E8

HI, LO = 0, 1
THREE = ((HI, HI), (HI, LO), (LO, HI))


def build(nc, a, scratch, out):
    fp32, f32r, bf16 = mybir.dt.float32, mybir.dt.float32r, mybir.dt.bfloat16
    i32, u32 = mybir.dt.int32, mybir.dt.uint32
    ALU = mybir.AluOpType
    ACT = mybir.ActivationFunctionType
    X = mybir.AxisListType.X
    ds = bass.ds

    top = [16512]

    def place(size):
        at = top[0]
        top[0] += -(-size // 32) * 32
        return at

    def sb(name, shape, dt, at=None):
        size = 4
        for n in shape[1:]:
            size *= n
        if dt == bf16:
            size //= 2
        return nc.alloc_sbuf_tensor_at(name, shape, dt, offset=place(size) if at is None else at)

    X0 = top[0]
    x_hl = [sb(f"x_hl{n}", [P, 2, KT, NB], f32r) for n in range(NH)]
    x_raw = sb("x_raw", [P, KT, T], fp32)
    W0 = top[0]
    ad_raw = sb("ad_raw", [P, BATCH, FT * RANK], fp32)
    wg_raw = sb("wg_raw", [P, 2, 2 * H], fp32)
    wg_hl = sb("wg_hl", [P, 2, 2, 2 * H], f32r)
    wd_raw = sb("wd_raw", [P, 2, H], fp32)
    wd_hl = sb("wd_hl", [P, 2, 2, H], f32r)
    b_raw = sb("b_raw", [P, 2, 2, 2 * P], fp32)
    b_hl = sb("b_hl", [P, 2, 2, 2, 2 * P], f32r)
    W1 = top[0]
    A0 = top[0]
    sil = sb("sil", [P, NB], fp32)
    act_raw = sb("act_raw", [P, NB], fp32)
    act_hl = sb("act_hl", [P, 2, 2, NB], f32r)
    ad_hl = sb("ad_hl", [P, 2, 2, HB * RANK], f32r)
    A1 = top[0]
    tg_hl = sb("tg_hl", [P, NH, 2, 2, NB], f32r)
    G0 = top[0]
    tg_tmp = sb("tg_tmp", [P, 2, NB], fp32)
    Y0 = top[0]
    y_hl = sb("y_hl", [P, 2, KT, NB], f32r)
    we_hl = sb("we_hl", [P, 2, KT, H], f32r)
    Y1 = top[0]
    D0 = top[0]
    td_raw = sb("td_raw", [P, NB], fp32)
    td_hl = sb("td_hl", [P, 2, NB], f32r)
    bd_hl = sb("bd_hl", [P, 2, 2, H], f32r)
    D1 = top[0]
    consts = sb("consts", [P, CONSTS], fp32)
    smalls = consts[:, 0:17]
    pat = consts[:, 17:C_FIRST].rearrange("p (f g) -> p f g", g=4)
    masks = consts[:, C_FIRST:C_FIRST + GT + P]
    ident = consts[:, C_FIRST + GT + P:C_FIRST + GT + 2 * P]
    iota_e = consts[:, C_FIRST + GT + 2 * P:CONSTS].rearrange("p (t e) -> p t e", e=E8)
    identb = sb("identb", [P, P], bf16)
    ints = sb("ints", [P, BATCH + 4 + TILES], i32)
    lang = ints[:, BATCH + 4:BATCH + 4 + TILES]
    ex_f = sb("ex_f", [P, BATCH + 4], fp32)
    ex_g = sb("ex_g", [P, BATCH + 4], fp32)
    ex_i = sb("ex_i", [P, BATCH], i32)
    idx_a = sb("idx_a", [P, BATCH], i32)
    idx_all = sb("idx_all", [P, FT, 4], i32)
    wm = sb("wm", [P, FT, 2], fp32)
    wdm = sb("wdm", [P, FT, 4], fp32)
    ws_all = sb("ws_all", [P, 2 * 2 * FT + 2 * 4], fp32)
    ws_t = sb("ws_t", [2 * 2 * FT + 8, P], fp32)
    ssq = sb("ssq", [P, TILES], fp32)
    qs = sb("qs", [P, 8, TILES], fp32)
    half = sb("half", [P, 1], fp32)
    warm = sb("warm", [P, 2], fp32)

    assert top[0] <= 229344, top[0]

    vu_raw = sb("vu_raw", [P, WCH, 2 * H], fp32, at=X0 + 4 * 2 * KT * NB)
    agu = sb("agu", [P, BATCH, 2 * KT * RANK], fp32, at=Y0)
    ag = [sb(f"ag{n}", [P, KT, KT, P], fp32, at=at) for n, at in enumerate((A0, Y0))]
    vr_raw = sb("vr_raw", [P, H], fp32, at=D0)
    vr_hl = sb("vr_hl", [P, H], f32r, at=D0 + 2048)
    c_hl = sb("c_hl", [P, H], f32r, at=D0 + 4096)
    ur = sb("ur", [4, H], fp32, at=D0 + 6144)
    bd_raw = sb("bd_raw", [P, 2, H], fp32, at=G0)
    nat = sb("nat", [P, 2, 3 * H], fp32, at=X0)
    x1_hl = sb("x1_hl", [P, 2, KT, T], f32r, at=X0)
    t_raw = [sb(f"t_raw{i}", [P, FP], fp32, at=at) for i, at in enumerate((W0, W0 + 4 * FP, D0 + 8704))]
    assert D0 + 8704 + 4 * FP <= D1
    at = W0 + 2 * FP * 4
    inv_b = sb("inv_b", [P, 2, F], fp32, at=at)
    ws_b = sb("ws_b", [P, 2, F], fp32, at=at + 8 * F)
    invd_b = sb("invd_b", [P, H], fp32, at=at + 16 * F)
    wsd_b = sb("wsd_b", [P, H], fp32, at=at + 16 * F + 2048)
    wq = sb("wq", [P, 2, KT, F], bf16, at=at + 16 * F + 4096)
    wqd_at = at + 16 * F + 4096 + 2 * KT * F * 2
    wqd = sb("wqd", [P, FT, H], bf16, at=wqd_at)
    assert wqd_at + FT * H * 2 <= W1
    wc_raw = sb("wc_raw", [P, KT, H], fp32, at=A1)
    bc_raw = sb("bc_raw", [P, H], fp32, at=wqd_at)
    wc_lo_hi = sb("wc_lo_hi", [P, 2, KT, H], f32r, at=A1)
    wc_hl = (wc_lo_hi[:, 1], wc_lo_hi[:, 0])
    awr = sb("awr", [P, KT, HT], fp32, at=A0)
    bc_hl = sb("bc_hl", [P, 2, H], f32r, at=A0 + 2176)
    rmsw = sb("rmsw", [P, H], fp32, at=A0 + 6272)
    h_sb = sb("h_sb", [P, TILES, HT], fp32, at=A0 + 8320)
    g_at = A0 + 12672
    lg = sb("lg", [P, TILES, E8], fp32, at=g_at)
    mx = sb("mx", [P, TILES, E8], fp32, at=g_at + 256)
    mi = sb("mi", [P, TILES, E8], u32, at=g_at + 512)
    oh = sb("oh", [P, 2, TILES, E8], fp32, at=g_at + 768)
    gates = sb("gates", [P, TILES, E8], fp32, at=g_at + 1280)
    gw = sb("gw", [P, 6, TILES], fp32, at=g_at + 1536)
    assert g_at + 1536 + 192 <= A1
    x1t = sb("x1t", [P, TILES, H], fp32, at=Y0)
    hgt_hl = sb("hgt_hl", [P, 2, T], f32r, at=Y0 + 16384)
    qt = sb("qt", [P, TILES, KT, P], bf16, at=Y0 + 24576)
    cw = sb("cw", [P, 2, H], fp32, at=D0)
    sq_junk = sb("sq_junk", [P, H], fp32, at=D0 + 4096)
    q1 = sb("q1", [P, 2, H], bf16, at=D0 + 6144)
    g_sb = sb("g_sb", [P, 2, F], fp32, at=X0)
    u_sb = sb("u_sb", [P, 2, F], fp32, at=X0 + 8 * F)
    h_rnd = sb("h_rnd", [P, F], fp32, at=X0 + 16 * F)
    q2 = sb("q2", [P, 2, F], bf16, at=X0 + 20 * F)
    q2t = sb("q2t", [P, 2, FT, P], bf16, at=X0 + 24 * F)
    o_sb = sb("o_sb", [P, 2, H], fp32, at=X0 + 24 * F + 5632)
    r_sb = sb("r_sb", [P, 2, H], fp32, at=X0 + 24 * F + 9728)
    assert X0 + 24 * F + 9728 + 4096 <= W0

    s_at = {"sall": slice(0, 4), "alpha": slice(4, 5), "beta": slice(5, 6), "s_r": slice(6, 7),
            "d": slice(7, 8), "bias": slice(8, 12), "r": slice(12, 16)}

    def hf(t):
        return t.bitcast(fp32)

    with ExitStack() as ctx:
        def sem(name):
            return ctx.enter_context(nc.semaphore(name))

        ps = [ctx.enter_context(nc.psum_tensor(f"ps{i}", [P, NB], fp32)) for i in range(8)]
        psb = [p[:].bitcast(bf16) for p in ps]
        GATE, TD = 5, 4
        CB = (0, 1, 3, 2)
        UP = (6, 7)

        small_in, it_in, const_in, vr_in, ur_in, bd_in = map(sem, (
            "small_in", "it_in", "const_in", "vr_in", "ur_in", "bd_in"))
        x_in = [sem(f"x_in{i}") for i in range(3)]
        vu_in = [sem(f"vu_in{c}") for c in range(WCH)]
        agu_in = [sem("agu_in0"), sem("agu_in1")]
        ad_in = [sem("ad_in0"), sem("ad_in1")]
        wg_in = [sem("wg_in0"), sem("wg_in1")]
        wd_in = [sem("wd_in0"), sem("wd_in1")]
        b_in = [sem("b_in0"), sem("b_in1")]
        nat_in = [sem("nat_in0"), sem("nat_in1")]
        t_in = [sem(f"t_in{i}") for i in range(3)]
        wc_in, bc_in, awr_in, rmsw_in, wsb_in, invb_in0 = map(sem, (
            "wc_in", "bc_in", "awr_in", "rmsw_in", "wsb_in", "invb_in0"))
        invb_in = [invb_in0, sem("invb_in1"), sem("invb_in2")]
        u_scaled, x_hi, x_lo, wg_hi, wg_lo, wd_hi, wd_lo, b_hi, b_lo, ad_hi, ad_lo, bd_hi, bd_lo = map(sem, (
            "u_scaled", "x_hi", "x_lo", "wg_hi", "wg_lo", "wd_hi", "wd_lo", "b_hi", "b_lo", "ad_hi", "ad_lo",
            "bd_hi", "bd_lo"))
        wg_used, down_done = sem("wg_used"), sem("down_done")
        idx_ready, vr_ready, urs_ready = map(sem, ("idx_ready", "vr_ready", "urs_ready"))
        cmix_ready, c_zero, c_hi, c_ready, we_ready, we_hi, we_lo = map(sem, (
            "cmix_ready", "c_zero", "c_hi", "c_ready", "we_ready", "we_hi", "we_lo"))
        tg_ready, tg_zero, tg_masked, tg_hi, tg_lo = map(sem, ("tg_ready", "tg_zero", "tg_masked", "tg_hi", "tg_lo"))
        gate_ready, silu_done, act_made, act_hi, act_lo = map(sem, (
            "gate_ready", "silu_done", "act_made", "act_hi", "act_lo"))
        td_masked, td_hi, td_lo, y_ready, y_hi, y_lo = map(sem, (
            "td_masked", "td_hi", "td_lo", "y_ready", "y_hi", "y_lo"))
        z_ready, x1_made, x1_hi, x1_lo = map(sem, ("z_ready", "x1_made", "x1_hi", "x1_lo"))
        nat_used, ws_made, wst_ready, wst_out, scr_out, iv = map(sem, (
            "nat_used", "ws_made", "wst_ready", "wst_out", "scr_out", "iv"))
        t_scaled, t_quant = sem("t_scaled"), sem("t_quant")
        wc_hi, wc_lo, bc_hi, bc_lo = map(sem, ("wc_hi", "wc_lo", "bc_hi", "bc_lo"))
        h_ready, h_out, x1t_ready, x1t_out = map(sem, ("h_ready", "h_out", "x1t_ready", "x1t_out"))
        diff_made, exp_made, hg_made, hgt_ready, hgt_hi, hgt_lo = map(sem, (
            "diff_made", "exp_made", "hg_made", "hgt_ready", "hgt_hi", "hgt_lo"))
        cond_ready, cw_made, max_made, sq_made, rs_made, q1_scaled, q1_made, qt_ready, qt_out = map(sem, (
            "cond_ready", "cw_made", "max_made", "sq_made", "rs_made", "q1_scaled", "q1_made", "qt_ready", "qt_out"))
        gq_ready, uq_ready, g_made, u_made, sg_made, h_made, h_scaled, q2_made = map(sem, (
            "gq_ready", "uq_ready", "g_made", "u_made", "sg_made", "h_made", "h_scaled", "q2_made"))
        hq, q2t_ready, q2t_out, o_ready, o_made, r_made = map(sem, ("hq", "q2t_ready", "q2t_out", "o_ready", "o_made", "r_made"))
        out_done = [sem("out_done0"), sem("out_done1")]
        dve_step, pool_step, ag_made = sem("dve_step"), sem("pool_step"), sem("ag_made")
        ident_b, warmed = sem("ident_b"), sem("warmed")

        block = ctx.enter_context(nc.Block())

        @block.sync
        def _(sp):
            sp.dma_start(ints[:], a["ints"]).then_inc(it_in, 16)
            sp.dma_start(consts[:, 0:C_FIRST], a["consts"][:, 0:C_FIRST]).then_inc(small_in, 16)
            for c in range(WCH - 1):
                sp.dma_start(vu_raw[:, c, :], a["w_vu"][c]).then_inc(vu_in[c], 16)
                if c >= 1:
                    k = 2 * (c - 1)
                    sp.dma_start(x_raw[:, k:k + 2, 0:NB], a["x_t"][:, k:k + 2, 0:NB]).then_inc(x_in[c - 1], 16)

            def load_wg(s, slot, src):
                sp.wait_ge(wg_hi, WCH + s - 1)
                sp.wait_ge(wg_lo, WCH + s - 1)
                sp.dma_start(wg_raw[:, slot, :], src).then_inc(wg_in[slot], 16)

            def load_wd(s, slot, src):
                sp.wait_ge(wd_hi, s - 1)
                sp.wait_ge(wd_lo, s - 1)
                sp.dma_start(wd_raw[:, slot, :], src).then_inc(wd_in[slot], 16)

            def load_nat(s, slot, src):
                sp.wait_ge(nat_used, s - 1)
                sp.dma_start(nat[:, slot, :], src).then_inc(nat_in[slot], 16)

            for s in range(2):
                sp.dma_start(wg_raw[:, s, :], a["w_gu"][s]).then_inc(wg_in[s], 16)
                sp.dma_start(wd_raw[:, s, :], a["w_d"][s]).then_inc(wd_in[s], 16)
                if s == 0:
                    sp.dma_start(vu_raw[:, WCH - 1, :], a["w_vu"][WCH - 1]).then_inc(vu_in[WCH - 1], 16)
                    sp.dma_start(consts[:, C_FIRST:CONSTS], a["consts"][:, C_FIRST:CONSTS]).then_inc(const_in, 16)
            sp.wait_ge(idx_ready, 1)
            with sp.Fori(0, HB) as b:
                e = sp.value_load(ex_i[0:1, ds(b, 1)], min_val=0, max_val=EXPERTS - 1)
                sp.dma_start(ad_raw[:, b, :], a["a_d"][e]).then_inc(ad_in[0], 16)
            sp.dma_start(x_raw[:, :, NB:T], a["x_t"][:, :, NB:T]).then_inc(x_in[2], 16)

            for n in range(NH):
                def step(f, par):
                    s, slot = n * FT + f, (n + par) % 2
                    load_wg(s, slot, a["w_gu"][f])
                    load_wd(s, slot, a["w_d"][f])
                    if n == 1:
                        load_nat(f, par, a["w_nat"][f])

                if n == 1:
                    for f in range(2):
                        s, slot = n * FT + f, (n + f) % 2
                        load_wg(s, slot, a["w_gu"][f])
                        load_wd(s, slot, a["w_d"][f])
                    sp.wait_ge(wg_used, WCH + FT)
                    for f in range(2):
                        sp.dma_start(nat[:, f, :], a["w_nat"][f]).then_inc(nat_in[f], 16)
                step(2, 0)
                if n == 1:
                    sp.dma_start(wc_raw[:], a["wc_t"]).then_inc(wc_in, 16)
                    sp.wait_ge(ad_hi, FT)
                    sp.wait_ge(ad_lo, FT)
                    for k in range(2):
                        sp.dma_start(t_raw[k][:, 0:F], a["wg_t"][k]).then_inc(t_in[k], 16)
                with sp.Fori(0, (FT - 3) // 2) as j:
                    step(2 * j + 3, 1)
                    step(2 * j + 4, 0)

            sp.wait_ge(wst_out, 1)
            sp.dma_start(scratch, ws_t[:]).then_inc(scr_out, 16)
            sp.wait_ge(wg_used, WCH + STEPS)
            sp.wait_ge(down_done, STEPS)
            sp.dma_start(awr[:], a["awr"]).then_inc(awr_in, 16)
            sp.wait_ge(scr_out, 16)
            sp.wait_ge(ad_hi, STEPS)
            sp.wait_ge(ad_lo, STEPS)
            for gu in range(2):
                r = 2 * FT + gu * FT
                sp.dma_start(inv_b[:, gu, :], scratch[r:r + FT, :].rearrange("(o f) p -> o (f p)", o=1)[:, 0:F]
                             .broadcast_to([P, F])).then_inc(invb_in[gu], 16)
            sp.dma_start(bc_raw[:], a["bc"]).then_inc(bc_in, 16)

            def load_t(c):
                if c < 8:
                    dst, src = t_raw[c % 3][:, 0:F], a["wg_t" if c < 4 else "wu_t"][c % 4]
                else:
                    f, w = 2 * (c - 8), min(2, FT - 2 * (c - 8))
                    dst = t_raw[c % 3][:, 0:w * H].rearrange("p (w h) -> p w h", w=w)
                    src = a["wd_t"][:, f:f + w, :]
                sp.dma_start(dst, src).then_inc(t_in[c % 3], 16)

            sp.wait_ge(y_ready, 2 * KT)
            load_t(2)
            sp.dma_start(rmsw[:], a["rmsw"]).then_inc(rmsw_in, 16)
            for c in range(3, 14):
                sp.wait_ge(t_quant, c - 2)
                load_t(c)
                if c == 5:
                    sp.dma_start(invd_b[:], scratch[4 * FT + 4:4 * FT + 8, :].rearrange("(o f) p -> o (f p)", o=1)
                                 .broadcast_to([P, H])).then_inc(invb_in[2], 16)
            for gu in range(2):
                r = gu * FT
                sp.dma_start(ws_b[:, gu, :], scratch[r:r + FT, :].rearrange("(o f) p -> o (f p)", o=1)[:, 0:F]
                             .broadcast_to([P, F])).then_inc(wsb_in, 16)
            sp.dma_start(wsd_b[:], scratch[4 * FT:4 * FT + 4, :].rearrange("(o f) p -> o (f p)", o=1)
                         .broadcast_to([P, H])).then_inc(wsb_in, 16)

            def store(t, slot):
                sp.wait_ge(r_made, t + 1)
                sp.dma_start(out[t], r_sb[:, slot, :]).then_inc(out_done[slot], 16)

            with sp.Fori(0, TILES // 2) as j:
                store(2 * j, 0)
                store(2 * j + 1, 1)
            for slot in range(2):
                sp.wait_ge(out_done[slot], 16 * TILES // 2)

        @block.gpsimd
        def _(gp):
            nc.gpsimd.memset(half[:], -0.5).then_inc(pool_step, 1)
            gp.wait_ge(pool_step, 1)

            def gather_a(table, tile, b, done):
                gp.indirect_dma_start(
                    out=tile[:, b, :], out_offset=None, in_=a[table].rearrange("e p c -> (e p) c"),
                    in_offset=bass.IndirectOffsetOnAxis(ap=idx_a[:, b:b + 1], axis=0),
                ).then_inc(done, 16)

            def gather_b(s):
                n, f = divmod(s, FT)
                slot = s % 2
                if s >= 2:
                    gp.wait_ge(b_hi, s - 1)
                    gp.wait_ge(b_lo, s - 1)
                for g in range(2):
                    gp.indirect_dma_start(
                        out=b_raw[:, slot, g, :], out_offset=None, in_=a["b_gu"],
                        in_offset=bass.IndirectOffsetOnAxis(ap=idx_all[:, f, 2 * n + g:2 * n + g + 1], axis=0),
                    ).then_inc(b_in[slot], 16)

            def gather_bd(n):
                if n == 0:
                    gp.wait_ge(tg_hi, NH)
                    gp.wait_ge(tg_lo, NH)
                else:
                    gp.wait_ge(bd_hi, n)
                    gp.wait_ge(bd_lo, n)
                for g in range(2):
                    gp.indirect_dma_start(
                        out=bd_raw[:, g, :], out_offset=None, in_=a["b_d"],
                        in_offset=bass.IndirectOffsetOnAxis(ap=idx_all[:, 0, 2 * n + g:2 * n + g + 1], axis=0),
                    ).then_inc(bd_in, 16)

            gp.wait_ge(idx_ready, 1)
            for b in range(HB):
                gather_a("a_gu", agu, b, agu_in[0])
            for s in range(STEPS):
                gather_b(s)
                if 2 <= s < 6:
                    for b in range(4 * s - 8, 4 * s - 4):
                        gather_a("a_gu", agu, HB + b, agu_in[1])
                if 6 <= s < 10:
                    for b in range(4 * s - 24, 4 * s - 20):
                        gather_a("a_d", ad_raw, HB + b, ad_in[1])
                if s == FT + 1:
                    gather_bd(0)
            gather_bd(1)

            def rms_scale(t):
                gp.wait_ge(cw_made, t + 1)
                nc.gpsimd.tensor_tensor(qs[:, 2, t:t + 1], qs[:, 0, t:t + 1], half[:], ALU.pow).then_inc(rs_made, 1)

            for c in range(14):
                if c >= 8:
                    rms_scale(c - 8)
                gp.wait_ge(t_in[c % 3], 16 * (c // 3 + 1))
                gp.wait_ge(invb_in[0 if c < 4 else 1 if c < 8 else 2], 16)
                if c < 8:
                    src, by = t_raw[c % 3][:, 0:F], inv_b[:, c // 4, :]
                else:
                    w = min(2, FT - 2 * (c - 8))
                    src = t_raw[c % 3][:, 0:w * H].rearrange("p (w h) -> p w h", w=w)
                    by = invd_b[:].unsqueeze(1).broadcast_to([P, w, H])
                nc.gpsimd.tensor_tensor(src, src, by, ALU.mult).then_inc(t_scaled, 1)

            for t in range(14 - 8, TILES):
                rms_scale(t)

            def h_mul(t, slot):
                gp.wait_ge(sg_made, t + 1)
                gp.wait_ge(u_made, 3 * t + 3)
                nc.gpsimd.tensor_tensor(g_sb[:, slot, :], g_sb[:, slot, :], u_sb[:, slot, :], ALU.mult).then_inc(h_made, 1)

            def residual(t, slot):
                gp.wait_ge(o_made, t + 1)
                gp.wait_ge(x1t_out, TILES)
                if not (isinstance(t, int) and t < 2):
                    gp.wait_ge(out_done[slot], 8 * (t - slot))
                nc.gpsimd.tensor_tensor(r_sb[:, slot, :], o_sb[:, slot, :], x1t[:, t, :], ALU.add).then_inc(r_made, 1)

            for t in range(2):
                h_mul(t, t)
            for t in (2, 3):
                h_mul(t, t % 2)
                residual(t - 2, t % 2)
            with gp.Fori(0, TILES // 2 - 2) as j:
                for d in range(2):
                    h_mul(2 * j + 4 + d, d)
                    residual(2 * j + 2 + d, d)
            for t in (6, 7):
                residual(t, t % 2)

        @block.scalar
        def _(act):
            def copy(o, i):
                return nc.scalar.activation(o, i, ACT.Copy)

            act.dma_start(ur[:], a["ur"]).then_inc(ur_in, 16)
            act.dma_start(vr_raw[:], a["vr"]).then_inc(vr_in, 16)
            act.wait_ge(pool_step, 1)
            nc.scalar.activation(warm[:, 0:1], half[:], ACT.Silu).then_inc(warmed, 1)

            def vu_split(c, slot):
                act.wait_ge(vu_in[c], 16)
                act.wait_ge(u_scaled, c + 1)
                if c >= 2:
                    act.wait_ge(wg_used, c - 1)
                copy(wg_hl[:, slot, HI, :], vu_raw[:, c, :]).then_inc(wg_hi, 1)

            def wg_split(s, slot):
                act.wait_ge(wg_in[slot], 8 * (s - slot) + 16)
                act.wait_ge(wg_used, WCH + s - 1)
                copy(wg_hl[:, slot, HI, :], wg_raw[:, slot, :]).then_inc(wg_hi, 1)

            def b_split(s, slot):
                act.wait_ge(b_in[slot], 16 * (s - slot) + 32)
                copy(b_hl[:, slot, HI, :, :], b_raw[:, slot, :, :]).then_inc(b_hi, 1)

            def ad_split(s, slot, f, n):
                copy(ad_hl[:, slot, HI, :].rearrange("p (b r) -> p b r", b=HB),
                     ad_raw[:, n * HB:(n + 1) * HB, ds(f * RANK, RANK)]).then_inc(ad_hi, 1)

            def wd_split(s, slot):
                act.wait_ge(wd_in[slot], 8 * (s - slot) + 16)
                copy(wd_hl[:, slot, HI, :], wd_raw[:, slot, :]).then_inc(wd_hi, 1)

            vu_split(0, 0)
            vu_split(1, 1)
            act.wait_ge(vr_in, 16)
            copy(vr_hl[:], vr_raw[:]).then_inc(vr_ready, 1)
            vu_split(2, 0)
            for i in range(2):
                act.wait_ge(x_in[i], 16)
                copy(x_hl[0][:, HI, 2 * i:2 * i + 2], x_raw[:, 2 * i:2 * i + 2, 0:NB]).then_inc(x_hi, 1)
            act.wait_ge(cmix_ready, 1)
            act.wait_ge(c_zero, 1)
            copy(c_hl[0:4, :], ps[TD][0:4, :]).then_inc(c_hi, 1)
            copy(c_hl[64:68, :], ps[TD][0:4, :]).then_inc(c_hi, 1)
            wg_split(0, 0)
            vu_split(3, 1)
            b_split(0, 0)

            def tg_split(n):
                act.wait_ge(tg_masked, 4 * (n + 1))
                copy(tg_hl[:, n, HI], tg_tmp[:]).then_inc(tg_hi, 1)

            tg_split(0)

            wg_split(1, 1)
            b_split(1, 1)
            for i in range(KT):
                act.wait_ge(we_ready, i + 1)
                copy(we_hl[:, HI, i, :], ps[i][:]).then_inc(we_hi, 1)

            def silu(s):
                act.wait_ge(gate_ready, s + 1)
                if not (isinstance(s, int) and s < 1):
                    act.wait_ge(act_made, s)
                nc.scalar.activation(sil[:], ps[GATE][:], ACT.Silu).then_inc(silu_done, 1)

            def act_split(s, slot):
                act.wait_ge(act_made, s + 1)
                if not (isinstance(s, int) and s < 2):
                    act.wait_ge(down_done, s - 1)
                copy(act_hl[:, slot, HI, :], act_raw[:]).then_inc(act_hi, 1)

            def step(f, par, n, split_next=True):
                s, slot = n * FT + f, (n + par) % 2
                if split_next:
                    wg_split(s + 1, 1 - slot)
                    b_split(s + 1, 1 - slot)
                silu(s)
                if not (isinstance(s, int) and s < 2):
                    act.wait_ge(down_done, s - 1)
                ad_split(s, slot, f, n)
                wd_split(s, slot)
                act_split(s, slot)

            def bd_split(n):
                act.wait_ge(bd_in, 32 * (n + 1))
                if n:
                    act.wait_ge(y_ready, KT * n)
                copy(bd_hl[:, HI], bd_raw[:]).then_inc(bd_hi, 1)

            def y_out(n):
                for m in range(KT):
                    act.wait_ge(y_ready, KT * n + m + 1)
                    copy(y_hl[:, HI, m, :], ps[m][:]).then_inc(y_hi, 1)

            act.wait_ge(ad_in[0], 16 * HB)
            step(0, 0, 0, split_next=False)
            step(1, 1, 0)
            act.wait_ge(wg_lo, WCH)
            act.wait_ge(x_in[2], 16)
            copy(x_hl[1][:, HI], x_raw[:, :, NB:T]).then_inc(x_hi, 1)
            step(2, 0, 0)
            with act.Fori(0, (FT - 3) // 2) as j:
                step(2 * j + 3, 1, 0)
                step(2 * j + 4, 0, 0)
            tg_split(1)
            act.wait_ge(ad_in[1], 16 * HB)
            step(0, 0, 1)
            act.wait_ge(td_masked, 1)
            copy(td_hl[:, HI], td_raw[:]).then_inc(td_hi, 1)
            bd_split(0)
            step(1, 1, 1)
            y_out(0)
            step(2, 0, 1)
            with act.Fori(0, (FT - 5) // 2) as j:
                step(2 * j + 3, 1, 1)
                step(2 * j + 4, 0, 1)
            step(FT - 2, 1, 1)
            step(FT - 1, 0, 1, split_next=False)

            def x1_split(q):
                n, m = divmod(q, KT)
                act.wait_ge(x1_made, q + 1)
                copy(x1_hl[:, HI, m, n * NB:(n + 1) * NB], x_raw[:, m, n * NB:(n + 1) * NB]).then_inc(x1_hi, 1)

            act.wait_ge(wc_in, 16)
            act.wait_ge(wg_used, WCH + STEPS)
            copy(wc_hl[HI], wc_raw[:]).then_inc(wc_hi, 1)
            x1_split(0)
            act.wait_ge(wst_ready, 1)
            copy(ws_t[:], ps[7][0:2 * 2 * FT + 8, 0:P]).then_inc(wst_out, 1)
            x1_split(1)
            act.wait_ge(td_masked, 2)
            copy(td_hl[:, HI], td_raw[:]).then_inc(td_hi, 1)
            bd_split(1)
            x1_split(2)
            x1_split(3)
            y_out(1)
            def h_copy(i):
                bank, t0, nt = ((4, 0, 3), (3, 3, 3), (4, 6, 2))[i]
                act.wait_ge(h_ready, t0 + nt)
                copy(h_sb[:, t0:t0 + nt, :], ps[bank][:, 0:nt * HT].rearrange("p (t h) -> p t h", t=nt)).then_inc(h_out, 1)

            h_copy(0)

            def x1t_copy(t):
                act.wait_ge(x1t_ready, t + 1)
                copy(x1t[:, t, :], ps[(5, 6, 7)[t % 3]][:]).then_inc(x1t_out, 1)

            x1_split(4)
            act.wait_ge(bc_in, 16)
            copy(bc_hl[:, HI], bc_raw[:]).then_inc(bc_hi, 1)
            for q in range(5, 8):
                x1_split(q)
            for t in range(4):
                x1t_copy(t)
            h_copy(1)
            h_copy(2)
            nc.scalar.activation(warm[:, 1:2], half[:], ACT.Exp).then_inc(warmed, 1)
            act.wait_ge(diff_made, 1)
            nc.scalar.activation(gw[:, 1, :], gw[:, 0, :], ACT.Exp).then_inc(exp_made, 1)
            for t in range(4, TILES):
                x1t_copy(t)
            act.wait_ge(warmed, 2)
            nc.scalar.activation(warm[:, 1:2], half[:], ACT.Silu).then_inc(warmed, 1)
            for i in range(2):
                act.wait_ge(hgt_ready, i + 1)
                copy(hgt_hl[:, HI, i * NB:(i + 1) * NB], ps[5 + i][:]).then_inc(hgt_hi, 1)

            def q1_round(t):
                act.wait_ge(q1_scaled, t + 1)
                if t >= 2:
                    act.wait_ge(qt_ready, t - 1)
                nc.scalar.activation(q1[:, t % 2, :], cw[:, t % 2, :], ACT.Copy, bias=-ROUND).then_inc(q1_made, 1)

            def qt_copy(t):
                act.wait_ge(qt_ready, t + 1)
                copy(qt[:, t, :, :].rearrange("p k m -> p (k m)"), psb[(7, 6)[t % 2]][:, 0:H]).then_inc(qt_out, 1)

            for t in range(TILES):
                act.wait_ge(cond_ready, t + 1)
                if t:
                    act.wait_ge(sq_made, t)
                nc.scalar.activation(sq_junk[:], ps[CB[t % 4]][:], ACT.Square, accum_out=ssq[:, t:t + 1]).then_inc(sq_made, 1)
                if t >= 1:
                    q1_round(t - 1)
                if t >= 3:
                    qt_copy(t - 3)
            q1_round(TILES - 1)
            for t in range(TILES - 3, TILES):
                qt_copy(t)

            def l1_silu(t, slot):
                act.wait_ge(g_made, 3 * t + 3)
                nc.scalar.activation(g_sb[:, slot, :], g_sb[:, slot, :], ACT.Silu).then_inc(sg_made, 1)

            def q2_round(t, slot):
                act.wait_ge(h_scaled, t + 1)
                if not (isinstance(t, int) and t < 2):
                    act.wait_ge(q2t_ready, 2 * t - 2)
                nc.scalar.activation(q2[:, slot, :], h_rnd[:], ACT.Copy, bias=-ROUND).then_inc(q2_made, 1)

            def q2t_copy(t, slot):
                act.wait_ge(q2t_ready, 2 * t + 1)
                if not (isinstance(t, int) and t < 2):
                    act.wait_ge(o_ready, t - 1)
                copy(q2t[:, slot, 0:6, :], psb[6][:, 0:6 * P].rearrange("p (j m) -> p j m", j=6)).then_inc(q2t_out, 1)
                act.wait_ge(q2t_ready, 2 * t + 2)
                copy(q2t[:, slot, 6:10, :], psb[6][:, 0:4 * P].rearrange("p (j m) -> p j m", j=4))
                copy(q2t[0:FREM, slot, 10, :], psb[6][0:FREM, 4 * P:5 * P]).then_inc(q2t_out, 1)

            def l1_step(t, slot):
                q2t_copy(t - 2, slot)
                l1_silu(t, slot)
                q2_round(t - 1, 1 - slot)

            l1_silu(0, 0)
            l1_silu(1, 1)
            q2_round(0, 0)
            for t in (2, 3):
                l1_step(t, t % 2)
            with act.Fori(0, TILES // 2 - 2) as j:
                for d in range(2):
                    l1_step(2 * j + 4 + d, d)
            q2t_copy(TILES - 2, 0)
            q2_round(TILES - 1, 1)
            q2t_copy(TILES - 1, 1)

        @block.vector
        def _(dve):
            steps = [0]

            def link(ins):
                steps[0] += 1
                ins.then_inc(dve_step, 1)
                dve.wait_ge(dve_step, steps[0])

            V = nc.vector
            dve.wait_ge(it_in, 16)
            link(V.tensor_copy(ex_f[:], ints[:, 0:BATCH + 4]))
            link(V.tensor_scalar(ex_g[:], ex_f[:], 0.0, float(EXPERTS), ALU.is_lt, ALU.mult))
            link(V.tensor_tensor(ex_f[:], ex_f[:], ex_g[:], ALU.add))
            link(V.tensor_scalar(ex_f[:], ex_f[:], 0.0, float(EXPERTS - 1), ALU.max, ALU.min))
            V.tensor_copy(ex_i[:], ex_f[:, 0:BATCH])
            dve.wait_ge(small_in, 16)
            V.tensor_scalar(idx_a[:], ex_f[:, 0:BATCH], float(P), smalls[:, 16:17], ALU.mult, ALU.add)
            link(V.scalar_tensor_tensor(idx_all[:], ex_f[:, BATCH:BATCH + 4].unsqueeze(1).broadcast_to([P, FT, 4]),
                                        float(RANK), pat, ALU.mult, ALU.add))
            V.memset(ssq[:], 0.0).then_inc(idx_ready, 1)
            V.memset(tg_tmp[:], 0.0).then_inc(tg_zero, 1)
            V.memset(c_hl[:].bitcast(u32), 0).then_inc(c_zero, 1)
            link(V.tensor_scalar(smalls[0:64, 0:1], smalls[0:64, 0:1], smalls[0:64, s_at["alpha"]],
                                 smalls[0:64, s_at["beta"]], ALU.mult, ALU.add))
            link(V.tensor_scalar(smalls[0:64, 0:1], smalls[0:64, 0:1], 0.0, None, ALU.max))
            link(V.tensor_scalar(smalls[0:4, s_at["d"]], smalls[0:4, s_at["d"]], 0.0, smalls[0:4, s_at["s_r"]],
                                 ALU.max, ALU.mult))
            dve.wait_ge(ur_in, 16)
            V.tensor_scalar(ur[:], ur[:], smalls[0:4, s_at["d"]], None, ALU.mult).then_inc(urs_ready, 1)

            def lo(o, raw, hi):
                return V.tensor_tensor(o, raw, hf(hi), ALU.subtract)

            def vu_split(c, slot):
                dve.wait_ge(vu_in[c], 16)
                V.tensor_scalar(vu_raw[:, c, H:2 * H], vu_raw[:, c, H:2 * H], smalls[:, c:c + 1], None,
                                ALU.mult).then_inc(u_scaled, 1)
                dve.wait_ge(wg_hi, c + 1 if c < 3 else WCH + 1)
                lo(wg_hl[:, slot, LO, :], vu_raw[:, c, :], wg_hl[:, slot, HI, :]).then_inc(wg_lo, 1)

            def wg_split(s, slot):
                dve.wait_ge(wg_in[slot], 8 * (s - slot) + 16)
                dve.wait_ge(wg_hi, WCH if isinstance(s, int) and s < 1 else WCH + s + 1)
                lo(wg_hl[:, slot, LO, :], wg_raw[:, slot, :], wg_hl[:, slot, HI, :]).then_inc(wg_lo, 1)

            def b_split(s, slot):
                dve.wait_ge(b_hi, s + 1)
                lo(b_hl[:, slot, LO, :, :], b_raw[:, slot, :, :], b_hl[:, slot, HI, :, :]).then_inc(b_lo, 1)

            def ag_copy(n):
                dve.wait_ge(agu_in[n], 16 * HB)
                for j in range(KT):
                    b = n * HB + 4 * j
                    V.tensor_copy(ag[n][:, j].rearrange("p k (g b r) -> p (k g) b r", g=2, b=4),
                                  agu[:, b:b + 4, :].rearrange("p b (q r) -> p q b r", r=RANK)).then_inc(ag_made, 1)

            vu_split(0, 0)
            vu_split(1, 1)
            dve.wait_ge(vr_ready, 1)
            lo(vr_hl[64:P, :], vr_raw[64:P, :], vr_hl[64:P, :]).then_inc(vr_ready, 1)
            vu_split(2, 0)
            for i in range(2):
                k = slice(2 * i, 2 * i + 2)
                dve.wait_ge(x_hi, i + 1)
                lo(x_hl[0][:, LO, k], x_raw[:, k, 0:NB], x_hl[0][:, HI, k]).then_inc(x_lo, 1)
            dve.wait_ge(c_hi, 2)
            dve.wait_ge(cmix_ready, 1)
            V.tensor_tensor(c_hl[32:36, :], ps[TD][0:4, :], hf(c_hl[0:4, :]), ALU.subtract).then_inc(c_ready, 1)
            V.tensor_tensor(c_hl[96:100, :], ps[TD][0:4, :], hf(c_hl[0:4, :]), ALU.subtract).then_inc(c_ready, 1)
            wg_split(0, 0)
            ag_copy(0)
            vu_split(3, 1)
            dve.wait_ge(const_in, 16)
            V.tensor_copy(identb[:], ident).then_inc(ident_b, 1)
            b_split(0, 0)

            def tg_split(n):
                dve.wait_ge(tg_zero, 1)
                dve.wait_ge(tg_ready, n + 1)
                if n:
                    dve.wait_ge(tg_hi, n)
                    dve.wait_ge(tg_lo, n)
                for gu in range(2):
                    for par in range(2):
                        rows = slice(64 * gu, 64 * gu + 64)
                        V.tensor_tensor(
                            tg_tmp[64 * par:64 * par + 64, gu, :].rearrange("p (g t) -> p g t", t=P)[:, par::2, :],
                            ps[UP[1]][rows, :].rearrange("p (g t) -> p g t", t=P)[:, par::2, :],
                            masks[rows, GT:GT + P].unsqueeze(1).broadcast_to([64, 2, P]), ALU.mult).then_inc(tg_masked, 1)
                dve.wait_ge(tg_masked, 4 * (n + 1))
                dve.wait_ge(tg_hi, n + 1)
                lo(tg_hl[:, n, LO], tg_tmp[:], tg_hl[:, n, HI]).then_inc(tg_lo, 1)

            tg_split(0)

            wg_split(1, 1)
            b_split(1, 1)
            for i in range(KT):
                dve.wait_ge(we_hi, i + 1)
                lo(we_hl[:, LO, i, :], ps[i][:], we_hl[:, HI, i, :]).then_inc(we_lo, 1)

            def make_act(s, par):
                dve.wait_ge(silu_done, s + 1)
                dve.wait_ge(wg_used, WCH + s + 1)
                if not (isinstance(s, int) and s < 1):
                    dve.wait_ge(act_lo, s)
                V.tensor_tensor(act_raw[:], ps[UP[par]][:], sil[:], ALU.mult).then_inc(act_made, 1)

            def nat_max(f, par):
                dve.wait_ge(nat_in[par], 8 * (f - par) + 16)
                V.tensor_reduce(wm[:, f, :],
                                nat[:, par, 0:2 * H].rearrange("p (g h) -> p g h", g=2), X, ALU.max,
                                apply_absolute_value=True)
                V.tensor_reduce(wdm[:, f, :],
                                nat[:, par, 2 * H:3 * H].rearrange("p (g h) -> p g h", g=4), X, ALU.max,
                                apply_absolute_value=True).then_inc(nat_used, 1)

            def step(f, par, n, split_next=True, take_max=True):
                s, slot = n * FT + f, (n + par) % 2
                if split_next:
                    wg_split(s + 1, 1 - slot)
                    b_split(s + 1, 1 - slot)
                make_act(s, slot)
                dve.wait_ge(ad_hi, s + 1)
                lo(ad_hl[:, slot, LO, :].rearrange("p (b r) -> p b r", b=HB),
                   ad_raw[:, n * HB:(n + 1) * HB, ds(f * RANK, RANK)],
                   ad_hl[:, slot, HI, :].rearrange("p (b r) -> p b r", b=HB)).then_inc(ad_lo, 1)
                dve.wait_ge(wd_hi, s + 1)
                lo(wd_hl[:, slot, LO, :], wd_raw[:, slot, :], wd_hl[:, slot, HI, :]).then_inc(wd_lo, 1)
                dve.wait_ge(act_hi, s + 1)
                lo(act_hl[:, slot, LO, :], act_raw[:], act_hl[:, slot, HI, :]).then_inc(act_lo, 1)
                if n == 1 and take_max:
                    nat_max(f, par)

            def td_mask(n):
                dve.wait_ge(down_done, FT * (n + 1))
                if n:
                    dve.wait_ge(td_lo, n)
                V.tensor_tensor(td_raw[:].rearrange("p (g t) -> p g t", g=2),
                                ps[TD][:].rearrange("p (g t) -> p g t", g=2),
                                masks[:, 0:GT].unsqueeze(1).broadcast_to([P, 2, GT]), ALU.mult).then_inc(td_masked, 1)
                dve.wait_ge(td_hi, n + 1)
                lo(td_hl[:, LO], td_raw[:], td_hl[:, HI]).then_inc(td_lo, 1)
                dve.wait_ge(bd_hi, n + 1)
                lo(bd_hl[:, LO], bd_raw[:], bd_hl[:, HI]).then_inc(bd_lo, 1)

            def y_out(n):
                for m in range(KT):
                    dve.wait_ge(y_hi, KT * n + m + 1)
                    lo(y_hl[:, LO, m, :], ps[m][:], y_hl[:, HI, m, :]).then_inc(y_lo, 1)

            step(0, 0, 0, split_next=False)
            step(1, 1, 0)
            dve.wait_ge(x_hi, 3)
            lo(x_hl[1][:, LO], x_raw[:, :, NB:T], x_hl[1][:, HI]).then_inc(x_lo, 1)
            step(2, 0, 0)
            with dve.Fori(0, (FT - 5) // 2) as j:
                step(2 * j + 3, 1, 0)
                step(2 * j + 4, 0, 0)
            ag_copy(1)
            step(FT - 2, 1, 0)
            step(FT - 1, 0, 0)
            tg_split(1)
            step(0, 0, 1)
            td_mask(0)
            step(1, 1, 1, take_max=False)
            y_out(0)
            nat_max(1, 1)
            step(2, 0, 1)
            with dve.Fori(0, (FT - 5) // 2) as j:
                step(2 * j + 3, 1, 1)
                step(2 * j + 4, 0, 1)
            step(FT - 2, 1, 1)
            step(FT - 1, 0, 1, split_next=False)

            ZB = (5, 6, 7, 5, 5, 0, 1, 2)

            def x1_out(q):
                n, m = divmod(q, KT)
                here = x_raw[:, m, n * NB:(n + 1) * NB]
                dve.wait_ge(z_ready, q + 1)
                V.scalar_tensor_tensor(here, ps[ZB[q]][:], smalls[:, 8 + m:9 + m], here, ALU.add,
                                       ALU.add).then_inc(x1_made, 1)
                dve.wait_ge(x1_hi, q + 1)
                lo(x1_hl[:, LO, m, n * NB:(n + 1) * NB], here, x1_hl[:, HI, m, n * NB:(n + 1) * NB]).then_inc(x1_lo, 1)

            dve.wait_ge(nat_used, FT)
            NG = 2 * FT
            link(V.tensor_copy(ws_all[:, 0:NG].rearrange("p (g f) -> p g f", g=2), wm[:].rearrange("p f g -> p g f")))
            link(V.tensor_reduce(ws_all[:, 2 * NG:2 * NG + 4], wdm[:].rearrange("p f m -> p m f"), X, ALU.max))
            for o in (0, 2 * NG):
                w = NG if o == 0 else 4
                link(V.tensor_scalar(ws_all[:, o:o + w], ws_all[:, o:o + w], 1.0 / QMAX, Q_GUARD, ALU.mult, ALU.max))
                last = V.reciprocal(ws_all[:, o + w:o + 2 * w], ws_all[:, o:o + w])
                if o == 0:
                    link(last)
                else:
                    last.then_inc(ws_made, 1)
            dve.wait_ge(wc_hi, 1)
            lo(wc_hl[LO], wc_raw[:], wc_hl[HI]).then_inc(wc_lo, 1)
            x1_out(0)
            x1_out(1)
            td_mask(1)
            x1_out(2)
            x1_out(3)
            y_out(1)
            def t_round(c):
                dve.wait_ge(t_scaled, c + 1)
                if c < 8:
                    src, dst = t_raw[c % 3][:, 0:F], wq[:, c // 4, c % 4, :]
                else:
                    f, w = 2 * (c - 8), min(2, FT - 2 * (c - 8))
                    src = t_raw[c % 3][:, 0:w * H].rearrange("p (w h) -> p w h", w=w)
                    dst = wqd[:, f:f + w, :]
                V.tensor_scalar(dst, src, ROUND, ROUND, ALU.add, ALU.subtract).then_inc(t_quant, 1)

            x1_out(4)
            dve.wait_ge(bc_hi, 1)
            lo(bc_hl[:, LO], bc_raw[:], bc_hl[:, HI]).then_inc(bc_lo, 1)
            t_round(0)
            x1_out(5)
            t_round(1)
            x1_out(6)
            x1_out(7)
            t_round(2)
            t_round(3)

            L3 = [P, TILES, E8]
            link(V.tensor_tensor(oh[:, 0], iota_e, lang.unsqueeze(2).broadcast_to(L3), ALU.is_equal))
            t_round(4)
            dve.wait_ge(h_out, 3)
            link(V.scalar_tensor_tensor(lg[:], oh[:, 0], LANG_BIAS, h_sb[:, :, E8 * R8:HT], ALU.mult, ALU.add))
            for t in range(TILES):
                last = V.max(mx[:, t, :], lg[:, t, :])
            link(last)
            t_round(5)
            for t in range(TILES):
                last = V.max_index(mi[:, t, :], mx[:, t, :], lg[:, t, :])
            link(last)
            V.tensor_tensor(gw[:, 0, :], mx[:, :, 1], mx[:, :, 0], ALU.subtract).then_inc(diff_made, 1)
            for k in range(2):
                last = V.tensor_tensor(oh[:, k], iota_e, mi[:, :, k:k + 1].broadcast_to(L3), ALU.is_equal)
            link(last)
            dve.wait_ge(exp_made, 1)
            link(V.tensor_scalar(gw[:, 2, :], gw[:, 1, :], 1.0, None, ALU.add))
            link(V.reciprocal(gw[:, 3, :], gw[:, 2, :]))
            link(V.tensor_scalar(gw[:, 4, :], gw[:, 3, :], MOE_SCALE, None, ALU.mult))
            link(V.tensor_tensor(gw[:, 5, :], gw[:, 4, :], gw[:, 1, :], ALU.mult))
            for k in range(2):
                last = V.tensor_tensor(oh[:, k], oh[:, k], gw[:, 4 + k, :].unsqueeze(2).broadcast_to(L3), ALU.mult)
            link(last)
            link(V.tensor_tensor(gates[:], oh[:, 0], oh[:, 1], ALU.add))
            for i in range(2):
                hh = h_sb[:, 4 * i:4 * i + 4, 0:E8 * R8].rearrange("p t (e r) -> p t e r", e=E8)
                V.tensor_tensor(hh, hh, gates[:, 4 * i:4 * i + 4, :].unsqueeze(3).broadcast_to([P, 4, E8, R8]),
                                ALU.mult).then_inc(hg_made, 1)
            t_round(6)
            for i in range(2):
                dve.wait_ge(hgt_hi, i + 1)
                lo(hgt_hl[:, LO, i * NB:(i + 1) * NB], ps[5 + i][:], hgt_hl[:, HI, i * NB:(i + 1) * NB]).then_inc(hgt_lo, 1)

            def q1_range(t):
                dve.wait_ge(cond_ready, t + 1)
                dve.wait_ge(sq_made, t + 1)
                if t >= 2:
                    dve.wait_ge(q1_made, t - 1)
                link(V.tensor_tensor(cw[:, t % 2, :], ps[CB[t % 4]][:], rmsw[:], ALU.mult))
                V.tensor_scalar(qs[:, 0, t:t + 1], ssq[:, t:t + 1], 1.0 / H, RMS_EPS, ALU.mult, ALU.add).then_inc(cw_made, 1)
                V.tensor_reduce(qs[:, 1, t:t + 1], cw[:, t % 2, :], X, ALU.max, apply_absolute_value=True).then_inc(max_made, 1)

            def q1_scale(t):
                dve.wait_ge(max_made, t + 1)
                dve.wait_ge(rs_made, t + 1)
                link(V.tensor_scalar(qs[:, 3, t:t + 1], qs[:, 1, t:t + 1], qs[:, 2, t:t + 1], 1.0 / QMAX, ALU.mult, ALU.mult))
                link(V.tensor_scalar(qs[:, 4, t:t + 1], qs[:, 3, t:t + 1], Q_GUARD, None, ALU.max))
                link(V.reciprocal(qs[:, 5, t:t + 1], qs[:, 4, t:t + 1]))
                link(V.tensor_tensor(qs[:, 6, t:t + 1], qs[:, 5, t:t + 1], qs[:, 2, t:t + 1], ALU.mult))
                V.tensor_scalar(cw[:, t % 2, :], cw[:, t % 2, :], qs[:, 6, t:t + 1], ROUND, ALU.mult,
                                ALU.add).then_inc(q1_scaled, 1)

            dve.wait_ge(rmsw_in, 16)
            for t in range(TILES):
                q1_range(t)
                if t:
                    q1_scale(t - 1)
                if t < TILES - 1:
                    t_round(7 + t)
            q1_scale(TILES - 1)
            dve.wait_ge(wsb_in, 48)

            def gu_out(t, slot, c):
                cols = slice(CO[c], CO[c] + CH[c])
                if c == 0 and not (isinstance(t, int) and t < 2):
                    dve.wait_ge(h_scaled, t - 1)
                dve.wait_ge(gq_ready, 3 * t + c + 1)
                V.scalar_tensor_tensor(g_sb[:, slot, cols], ps[c][:, 0:CH[c]], qs[:, 4, ds(t, 1)], ws_b[:, 0, cols],
                                       ALU.mult, ALU.mult).then_inc(g_made, 1)
                dve.wait_ge(uq_ready, 3 * t + c + 1)
                V.scalar_tensor_tensor(u_sb[:, slot, cols], ps[3 + c][:, 0:CH[c]], qs[:, 4, ds(t, 1)], ws_b[:, 1, cols],
                                       ALU.mult, ALU.mult).then_inc(u_made, 1)

            def h_quant(t, slot):
                dve.wait_ge(h_made, t + 1)
                c0 = qs[:, 7, 4 * slot:4 * slot + 1]
                s2 = qs[:, 7, 4 * slot + 1:4 * slot + 2]
                i2 = qs[:, 7, 4 * slot + 2:4 * slot + 3]
                V.tensor_reduce(c0, g_sb[:, slot, :], X, ALU.max, apply_absolute_value=True).then_inc(hq, 1)
                dve.wait_ge(hq, 3 * t + 1)
                V.tensor_scalar(s2, c0, 1.0 / QMAX, Q_GUARD, ALU.mult, ALU.max).then_inc(hq, 1)
                dve.wait_ge(hq, 3 * t + 2)
                V.reciprocal(i2, s2).then_inc(hq, 1)
                if not (isinstance(t, int) and t < 1):
                    dve.wait_ge(q2_made, t)
                dve.wait_ge(hq, 3 * t + 3)
                V.tensor_scalar(h_rnd[:], g_sb[:, slot, :], i2, ROUND, ALU.mult, ALU.add).then_inc(h_scaled, 1)

            def o_out(t, slot):
                dve.wait_ge(o_ready, t + 1)
                if not (isinstance(t, int) and t < 2):
                    dve.wait_ge(r_made, t - 1)
                V.scalar_tensor_tensor(o_sb[:, slot, :], ps[7][:], qs[:, 7, 4 * slot + 1:4 * slot + 2], wsd_b[:],
                                       ALU.mult, ALU.mult).then_inc(o_made, 1)

            def l1_step(t, slot):
                for c in range(3):
                    gu_out(t, slot, c)
                h_quant(t - 1, 1 - slot)
                o_out(t - 2, slot)

            for t in range(2):
                for c in range(3):
                    gu_out(t, t, c)
            h_quant(0, 0)
            for t in (2, 3):
                l1_step(t, t % 2)
            with dve.Fori(0, TILES // 2 - 2) as j:
                for d in range(2):
                    l1_step(2 * j + 4 + d, d)
            h_quant(TILES - 1, 1)
            o_out(TILES - 2, 0)
            o_out(TILES - 1, 1)

        @block.tensor
        def _(pe):
            mm, tr = nc.tensor.matmul, nc.tensor.transpose

            def w_eff(c):
                slot = c % 2
                pe.wait_ge(wg_lo, c + 1 if c < WCH - 1 else WCH + 1)
                for i in range(KT):
                    for w, v in THREE:
                        last = mm(ps[i][:], wg_hl[:, slot, w, i * P:(i + 1) * P], wg_hl[:, slot, v, H:2 * H],
                                  start=(c == 0 and (w, v) == THREE[0]), stop=False)
                last.then_inc(wg_used, 1)

            def delta():
                pe.wait_ge(vr_ready, 2)
                pe.wait_ge(c_ready, 2)
                for i in range(KT):
                    mm(ps[i][:], vr_hl[:, i * P:(i + 1) * P], c_hl[:], start=False, stop=True).then_inc(we_ready, 1)

            def lora_in(n):
                pe.wait_ge(ag_made, KT * (n + 1))
                for i in ((0, 1), (2,))[n]:
                    pe.wait_ge(x_in[i], 16)
                for j in range(KT):
                    for k in range(KT):
                        last = mm(ps[UP[1]][:, j * P:(j + 1) * P], ag[n][:, j, k, :],
                                  x_raw[:, k, n * NB + j * P:n * NB + (j + 1) * P], start=(k == 0), stop=(k == KT - 1))
                last.then_inc(tg_ready, 1)

            def gate_up_base(bank, slot, n, gu, first=False):
                for k in range(KT):
                    if first and k % 2 == 0:
                        pe.wait_ge(x_lo, k // 2 + 1)
                    for w, v in THREE:
                        mm(bank[:], wg_hl[:, slot, w, gu * H + k * P:gu * H + (k + 1) * P], x_hl[n][:, v, k, :],
                           start=(k == 0 and (w, v) == THREE[0]), stop=False)

            def gate_up_lora(bank, slot, n, gu):
                for g in range(2):
                    for w, v in THREE:
                        last = mm(bank[:, g * GT:(g + 1) * GT], b_hl[:, slot, w, g, gu * P:(gu + 1) * P],
                                  tg_hl[:, n, v, gu, g * GT:(g + 1) * GT], start=False,
                                  stop=(g == 1 and (w, v) == THREE[-1]))
                last.then_inc(gate_ready if gu == 0 else wg_used, 1)

            def gate_up(s, slot, n, first=False):
                pe.wait_ge(wg_lo, WCH + s + 1)
                if not (isinstance(s, int) and s < 1):
                    pe.wait_ge(silu_done, s)
                gate_up_base(ps[GATE], slot, n, 0)
                pe.wait_ge(b_lo, s + 1)
                if first:
                    pe.wait_ge(tg_lo, n + 1)
                gate_up_lora(ps[GATE], slot, n, 0)
                if not (isinstance(s, int) and s < 2):
                    pe.wait_ge(act_made, s - 1)
                gate_up_base(ps[UP[slot]], slot, n, 1)
                gate_up_lora(ps[UP[slot]], slot, n, 1)

            def down(s, slot, n, first=False, end=False):
                pe.wait_ge(ad_lo, s + 1)
                pe.wait_ge(wd_lo, s + 1)
                pe.wait_ge(act_lo, s + 1)
                if first:
                    if n:
                        pe.wait_ge(td_masked, n)
                    else:
                        pe.wait_ge(we_lo, KT)
                for g in range(2):
                    for w, v in THREE:
                        mm(ps[TD][:, g * GT:(g + 1) * GT], ad_hl[:, slot, w, g * P:(g + 1) * P],
                           act_hl[:, slot, v, g * GT:(g + 1) * GT], start=(first and g == 0 and (w, v) == THREE[0]),
                           stop=(end and g == 1 and (w, v) == THREE[-1]), skip_group_check=True)
                for m in range(KT):
                    if first and n:
                        pe.wait_ge(y_lo, KT * (n - 1) + m + 1)
                    for w, v in THREE:
                        last = mm(ps[m][:], wd_hl[:, slot, w, m * P:(m + 1) * P], act_hl[:, slot, v, :],
                                  start=(first and (w, v) == THREE[0]), stop=False)
                last.then_inc(down_done, 1)

            def lora_down(n):
                pe.wait_ge(td_lo, n + 1)
                pe.wait_ge(bd_lo, n + 1)
                for m in range(KT):
                    for g in range(2):
                        for w, v in THREE:
                            last = mm(ps[m][:, g * GT:(g + 1) * GT], bd_hl[:, w, g, m * P:(m + 1) * P],
                                      td_hl[:, v, g * GT:(g + 1) * GT], start=False,
                                      stop=(g == 1 and (w, v) == THREE[-1]))
                    last.then_inc(y_ready, 1)

            for c in range(WCH - 1):
                w_eff(c)
                if c == 1:
                    pe.wait_ge(urs_ready, 1)
                    mm(ps[TD][0:4, :], smalls[0:4, s_at["r"]], ur[:], start=True, stop=True).then_inc(cmix_ready, 1)
            pe.wait_ge(wg_lo, WCH)
            gate_up_base(ps[GATE], 0, 0, 0, first=True)
            gate_up_base(ps[UP[0]], 0, 0, 1)
            lora_in(0)
            w_eff(WCH - 1)
            delta()
            pe.wait_ge(b_lo, 1)
            pe.wait_ge(tg_lo, 1)
            gate_up_lora(ps[GATE], 0, 0, 0)
            gate_up_lora(ps[UP[0]], 0, 0, 1)
            gate_up(1, 1, 0)
            down(0, 0, 0, first=True)
            gate_up(2, 0, 0)
            down(1, 1, 0)
            with pe.Fori(0, (FT - 5) // 2) as j:
                gate_up(2 * j + 3, 1, 0)
                down(2 * j + 2, 0, 0)
                gate_up(2 * j + 4, 0, 0)
                down(2 * j + 3, 1, 0)
            gate_up(FT - 2, 1, 0)
            down(FT - 3, 0, 0)
            gate_up(FT - 1, 0, 0)
            pe.wait_ge(act_made, FT - 1)
            lora_in(1)
            down(FT - 2, 1, 0)
            pe.wait_ge(x_lo, 3)
            gate_up(FT, 1, 1, first=True)
            down(FT - 1, 0, 0, end=True)
            gate_up(FT + 1, 0, 1)
            lora_down(0)
            down(FT, 1, 1, first=True)
            gate_up(FT + 2, 1, 1)
            down(FT + 1, 0, 1)
            with pe.Fori(0, (FT - 3) // 2) as j:
                gate_up(2 * j + FT + 3, 0, 1)
                down(2 * j + FT + 2, 1, 1)
                gate_up(2 * j + FT + 4, 1, 1)
                down(2 * j + FT + 3, 0, 1)

            ZB = (5, 6, 7, 5, 5, 0, 1, 2)

            def z(q):
                n, m = divmod(q, KT)
                pe.wait_ge(y_lo, KT * (n + 1))
                if q == 0:
                    pe.wait_ge(silu_done, STEPS)
                    pe.wait_ge(act_made, STEPS)
                if q in (3, 4):
                    pe.wait_ge(x1_made, 1 if q == 3 else 4)
                for k in range(KT):
                    for w, v in THREE:
                        last = mm(ps[ZB[q]][:], we_hl[:, w, k, m * P:(m + 1) * P], y_hl[:, v, k, :],
                                  start=(k == 0 and (w, v) == THREE[0]), stop=(k == KT - 1 and (w, v) == THREE[-1]))
                last.then_inc(z_ready, 1)

            def h_logits(t, bank, at):
                for k in range(KT):
                    last = mm(ps[bank][:, at * HT:(at + 1) * HT], x_raw[:, k, t * P:(t + 1) * P], awr[:, k, :],
                              start=(k == 0), stop=(k == KT - 1))
                last.then_inc(h_ready, 1)

            z(0)
            z(1)
            pe.wait_ge(ws_made, 1)
            pe.wait_ge(const_in, 16)
            tr(ps[7][0:2 * 2 * FT + 8, 0:P], ws_all[:], ident).then_inc(wst_ready, 1)
            down(STEPS - 1, 1, 1, end=True)
            pe.wait_ge(wst_out, 1)
            z(2)
            z(3)
            lora_down(1)
            pe.wait_ge(awr_in, 16)
            pe.wait_ge(x1_made, 4)
            for t in range(3):
                h_logits(t, 4, t)
            for q in range(4, 8):
                z(q)

            def x1_transpose(t):
                if t in (0, 1, 2):
                    pe.wait_ge(x1_made, 5)
                else:
                    pe.wait_ge(x1t_out, t - 2)
                for k in range(KT):
                    last = tr(ps[(5, 6, 7)[t % 3]][:, k * P:(k + 1) * P], x_raw[:, k, t * P:(t + 1) * P], ident)
                last.then_inc(x1t_ready, 1)

            for t in range(4):
                x1_transpose(t)
            pe.wait_ge(x1_made, 8)
            for t in range(3, 6):
                h_logits(t, 3, t - 3)
            pe.wait_ge(h_out, 1)
            for t in range(6, 8):
                h_logits(t, 4, t - 6)

            def cond(t):
                if t == 2:
                    pe.wait_ge(h_out, 2)
                if t >= 4:
                    pe.wait_ge(cw_made, t - 3)
                for k in range(KT):
                    for w, v in THREE:
                        mm(ps[CB[t % 4]][:], x1_hl[:, w, k, t * P:(t + 1) * P], wc_hl[v][:, k, :],
                           start=(k == 0 and (w, v) == THREE[0]), stop=False)

            def cond_lora(t):
                if t in (0, 4):
                    pe.wait_ge(hgt_lo, 1 + t // 4)
                for w, v in THREE:
                    last = mm(ps[CB[t % 4]][:], hgt_hl[:, w, t * P:(t + 1) * P], bc_hl[:, v, :], start=False,
                              stop=((w, v) == THREE[-1]))
                last.then_inc(cond_ready, 1)

            def qt_transpose(t):
                pe.wait_ge(q1_made, t + 1)
                if t == 1:
                    pe.wait_ge(hgt_lo, 2)
                if t >= 2:
                    pe.wait_ge(qt_out, t - 1)
                for k in range(KT):
                    last = tr(psb[(7, 6)[t % 2]][:, k * P:(k + 1) * P], q1[:, t % 2, k * P:(k + 1) * P], identb[:])
                last.then_inc(qt_ready, 1)

            pe.wait_ge(x1_lo, 8)
            pe.wait_ge(wc_lo, 1)
            pe.wait_ge(bc_lo, 1)
            pe.wait_ge(ident_b, 1)
            cond(0)
            for t in range(4, TILES):
                x1_transpose(t)
            cond(1)
            pe.wait_ge(x1t_out, TILES)
            for t in range(TILES):
                pe.wait_ge(hg_made, 1 + t // 4)
                last = tr(ps[5 + t // 4][:, (t % 4) * P:(t % 4 + 1) * P], h_sb[:, t, 0:E8 * R8], ident)
                if t % 4 == 3:
                    last.then_inc(hgt_ready, 1)
            cond(2)
            for t in range(3):
                cond_lora(t)
            for t in range(3, TILES):
                cond(t)
                cond_lora(t)
                qt_transpose(t - 3)
            qt_transpose(TILES - 3)

            def l1_gate_up(t, c):
                for gu, made in ((0, g_made), (1, u_made)):
                    if not (isinstance(t, int) and t < 1):
                        pe.wait_ge(made, 3 * t + c - 2)
                    for k in range(KT):
                        last = mm(ps[3 * gu + c][:, 0:CH[c]], qt[:, t, k, :], wq[:, gu, k, CO[c]:CO[c] + CH[c]],
                                  start=(k == 0), stop=(k == KT - 1))
                    last.then_inc((gq_ready, uq_ready)[gu], 1)

            def q2_transpose(t, slot, part):
                if part == 0:
                    pe.wait_ge(q2_made, t + 1)
                if not (isinstance(t, int) and t < 1 and part == 0):
                    pe.wait_ge(q2t_out, 2 * t + part)
                blocks = range(6) if part == 0 else range(6, FT)
                for i, j in enumerate(blocks):
                    m = min(P, F - j * P)
                    last = tr(psb[6][0:m, i * P:(i + 1) * P], q2[:, slot, j * P:j * P + m], identb[:])
                last.then_inc(q2t_ready, 1)

            def l1_down(t, slot):
                if not (isinstance(t, int) and t < 1):
                    pe.wait_ge(o_made, t)
                for j in range(FT):
                    if j in (0, 6):
                        pe.wait_ge(q2t_out, 2 * t + (1 if j == 0 else 2))
                    m = min(P, F - j * P)
                    last = mm(ps[7][:], q2t[0:m, slot, j, :], wqd[0:m, j, :], start=(j == 0), stop=(j == FT - 1))
                last.then_inc(o_ready, 1)

            def l1_step(t, slot):
                l1_gate_up(t, 0)
                l1_gate_up(t, 1)
                q2_transpose(t - 2, slot, 0)
                l1_gate_up(t, 2)
                q2_transpose(t - 2, slot, 1)
                l1_down(t - 2, slot)

            pe.wait_ge(t_quant, 8)
            pe.wait_ge(h_out, 3)
            pe.wait_ge(hgt_lo, 1)
            pe.wait_ge(qt_out, 1)
            for c in range(3):
                pe.wait_ge(cw_made, TILES if c == 2 else TILES - 1)
                l1_gate_up(0, c)
            qt_transpose(TILES - 2)
            qt_transpose(TILES - 1)
            for c in range(3):
                l1_gate_up(1, c)
            pe.wait_ge(qt_out, TILES)
            pe.wait_ge(t_quant, 14)
            for c in range(3):
                l1_gate_up(2, c)
            q2_transpose(0, 0, 0)
            q2_transpose(0, 0, 1)
            l1_down(0, 0)
            l1_step(3, 1)
            with pe.Fori(0, TILES // 2 - 2) as j:
                for d in range(2):
                    l1_step(2 * j + 4 + d, d)
            for t in (TILES - 2, TILES - 1):
                q2_transpose(t, t % 2, 0)
                q2_transpose(t, t % 2, 1)
                l1_down(t, t % 2)


def kernel(**inputs):
    import numpy as np
    import concourse.bacc as bacc
    from concourse.bass_utils import run_bass_kernel_spmd as run

    g = {k: np.asarray(v) for k, v in inputs.items()}

    def pad_f(w, axis):
        z = list(w.shape)
        z[axis] = FP - F
        return np.concatenate([w, np.zeros(z, w.dtype)], axis)

    wg, wu = pad_f(g["L0_cond_W_gate"], 0), pad_f(g["L0_cond_W_up"], 0)
    bg, bu = (pad_f(g[k][0], 1) for k in ("L0_cond_B_gate", "L0_cond_B_up"))
    ag, au = g["L0_cond_A_gate"][0], g["L0_cond_A_up"][0]
    smalls = np.zeros((P, 17), np.float32)
    smalls[:, 0:4] = np.concatenate([g["L0_ffn_S_top"], g["L0_ffn_S_tail"]]).reshape(KT, P).T
    smalls[0:64, 4] = g["L0_ffn_alpha"]
    smalls[0:64, 5] = g["L0_ffn_beta"]
    smalls[0:4, 6] = g["L0_ffn_S_tail_r"]
    smalls[0:4, 7] = g["L0_ffn_D"]
    smalls[:, 8:12] = g["L0_ffn_bias"].reshape(KT, P).T
    smalls[0:4, 12:16] = g["L0_ffn_R"]
    v_all = np.concatenate([g["L0_ffn_Vh_top"], g["L0_ffn_Vh_tail"]], 0).reshape(KT, P, H)
    ut_all = np.concatenate([g["L0_ffn_U_top"], g["L0_ffn_U_tail"]], 1).T.reshape(KT, P, H)
    p = np.arange(P)
    mask_b = (p[:, None] // RANK == np.arange(GT)[None, :] // SEQ)
    mask_q = ((p[:, None] % 64) // RANK == p[None, :] // SEQ)
    smalls[:, 16] = p
    pat = np.broadcast_to((p[:, None] % RANK + 2 * P * np.arange(FT)[None, :])[:, :, None], (P, FT, 4)).reshape(P, 4 * FT)
    iota = np.broadcast_to(np.arange(E8), (P, TILES, E8)).reshape(P, TILES * E8)
    consts = np.concatenate([smalls, pat, LORA_SCALE * np.concatenate([mask_b, mask_q], 1), np.eye(P), iota], 1)
    ids = g["itok_B_2_6"]
    ints = np.concatenate([np.broadcast_to(ids, (P, BATCH)), np.repeat(ids.reshape(4, GB), RANK, axis=1).T,
                           np.repeat(g["itok_B_0_7"].reshape(TILES, P // SEQ), SEQ, axis=1).T], 1)
    vr = np.zeros((4, 32, H), np.float32)
    vr[:, 0:4] = g["L0_ffn_Vh_tail_r"]
    l1g, l1u, l1d = g["L1_ffn_Wg"], g["L1_ffn_Wu"], g["L1_ffn_Wd"]
    arrays = {
        "x_t": g["x"].reshape(T, KT, P).transpose(2, 1, 0),
        "ints": ints.astype(np.int32),
        "consts": consts.astype(np.float32),
        "w_vu": np.concatenate([v_all, ut_all], 2),
        "vr": vr.reshape(P, H),
        "ur": g["L0_ffn_U_tail_r"].T,
        "w_gu": np.stack([wg, wu]).reshape(2, FT, P, KT, P).transpose(1, 4, 0, 3, 2).reshape(FT, P, 2 * H),
        "w_d": pad_f(g["L0_cond_W_down"], 1).T.reshape(FT, P, H),
        "a_gu": np.stack([ag, au]).reshape(2, EXPERTS, RANK, KT, P).transpose(1, 4, 3, 0, 2).reshape(EXPERTS, P, 2 * KT * RANK),
        "a_d": pad_f(g["L0_cond_A_down"][0], 2).reshape(EXPERTS, RANK, FT, P).transpose(0, 3, 2, 1).reshape(EXPERTS, P, FT * RANK),
        "b_gu": np.stack([bg, bu]).reshape(2, EXPERTS, FT, P, RANK).transpose(2, 1, 4, 0, 3).reshape(FT * EXPERTS * RANK, 2 * P),
        "b_d": g["L0_cond_B_down"][0].transpose(0, 2, 1).reshape(EXPERTS * RANK, H),
        "w_nat": np.concatenate([pad_f(l1g, 0).reshape(FT, P, H), pad_f(l1u, 0).reshape(FT, P, H),
                                 pad_f(l1d, 1).reshape(KT, P, FT, P).transpose(2, 1, 0, 3).reshape(FT, P, H)], 2),
        "wg_t": l1g.T.reshape(KT, P, F),
        "wu_t": l1u.T.reshape(KT, P, F),
        "wd_t": pad_f(l1d, 1).T.reshape(FT, P, H).transpose(1, 0, 2),
        "wc_t": g["L1_cond_W"].T.reshape(KT, P, H).transpose(1, 0, 2),
        "awr": np.concatenate([g["L1_cond_A"].reshape(E8 * R8, H), g["L1_cond_Wr"]], 0).T.reshape(KT, P, HT).transpose(1, 0, 2),
        "bc": g["L1_cond_B"].transpose(0, 2, 1).reshape(E8 * R8, H),
        "rmsw": np.broadcast_to(g["L1_ffn_rmsnorm_weight"], (P, H)),
    }
    arrays = {k: np.ascontiguousarray(v) for k, v in arrays.items()}
    nc = bacc.Bacc("TRN2", target_bir_lowering=False, num_devices=1)
    aps = {k: nc.dram_tensor(k + "_dram", v.shape, mybir.dt.from_np(v.dtype), kind="ExternalInput").ap()
           for k, v in arrays.items()}
    scratch = nc.dram_tensor("scale_scratch", [2 * 2 * FT + 8, P], mybir.dt.float32).ap()
    out = nc.dram_tensor("out_dram", [TILES, P, H], mybir.dt.float32, kind="ExternalOutput").ap()
    build(nc, aps, scratch, out)
    r = run(nc, [{k + "_dram": v for k, v in arrays.items()}], core_ids=[0])
    return r.results[0]["out_dram"].reshape(g["x"].shape)
```

```python
import concourse.bass as bass
from concourse import mybir
from contextlib import ExitStack

P = 128
T = 1024
H = 512
F = 1376
FT = 11
FP = FT * P
FREM = F - (FT - 1) * P
KT = H // P
HH = H // 2
NB = 512
NH = T // NB
BATCH, SEQ = 32, 32
EXPERTS, RANK = 16, 16
GB = P // RANK
GT = GB * SEQ
HB = BATCH // NH
E8, R8 = 8, 16
TILES = T // P
HT = E8 * R8 + E8
LORA_SCALE = 0.5
MOE_SCALE = 2.0
LANG_BIAS = 5.0
RMS_EPS = 1e-6
QMAX = 127.0
Q_GUARD = 1e-8
ROUND = 12582912.0
CH = (459, 459, 458)
CO = (0, 459, 918)
Q2_PARTS = (slice(0, 6 * P), slice(6 * P, F))
WCH = KT
STEPS = NH * FT
VU_SLOT = (0, 1, 1, 0)
VU_TURN = (1, 2, 4, 5)
STEP0_TURN = 3
C_FIRST = 17 + 4 * FT
CONSTS = C_FIRST + GT + 2 * P + TILES * E8

HI, LO = 0, 1
THREE = ((HI, HI), (HI, LO), (LO, HI))


def build(nc, a, scratch, out):
    fp32, f32r, bf16 = mybir.dt.float32, mybir.dt.float32r, mybir.dt.bfloat16
    i32, u32 = mybir.dt.int32, mybir.dt.uint32
    ALU = mybir.AluOpType
    ACT = mybir.ActivationFunctionType
    X = mybir.AxisListType.X
    ds = bass.ds

    top = [16512]

    def place(size):
        at = top[0]
        top[0] += -(-size // 32) * 32
        return at

    def sb(name, shape, dt, at=None):
        size = 4
        for n in shape[1:]:
            size *= n
        if dt == bf16:
            size //= 2
        return nc.alloc_sbuf_tensor_at(name, shape, dt, offset=place(size) if at is None else at)

    X0 = top[0]
    x_hl = [sb(f"x_hl{n}", [P, 2, KT, NB], f32r) for n in range(NH)]
    x_raw = sb("x_raw", [P, KT, T], fp32)
    W0 = top[0]
    ad_raw = sb("ad_raw", [P, BATCH, FT * RANK], fp32)
    wg_raw = sb("wg_raw", [P, 2, 2 * H], fp32)
    wg_hl = sb("wg_hl", [P, 2, 2, 2 * H], f32r)
    wd_raw = sb("wd_raw", [P, 2, H], fp32)
    wd_hl = sb("wd_hl", [P, 2, 2, H], f32r)
    b_raw = sb("b_raw", [P, 2, 2, 2 * P], fp32)
    b_hl = sb("b_hl", [P, 2, 2, 2, 2 * P], f32r)
    W1 = top[0]
    A0 = top[0]
    sil = sb("sil", [P, NB], fp32)
    act_raw = sb("act_raw", [P, NB], fp32)
    act_hl = sb("act_hl", [P, 2, 2, NB], f32r)
    ad_hl = sb("ad_hl", [P, 2, 2, HB * RANK], f32r)
    A1 = top[0]
    tg_hl = sb("tg_hl", [P, NH, 2, 2, NB], f32r)
    G0 = top[0]
    tg_tmp = sb("tg_tmp", [P, 2, NB], fp32)
    Y0 = top[0]
    y_hl = sb("y_hl", [P, 2, KT, NB], f32r)
    we_hl = sb("we_hl", [P, 2, KT, H], f32r)
    Y1 = top[0]
    D0 = top[0]
    td_raw = sb("td_raw", [P, NB], fp32)
    td_hl = sb("td_hl", [P, 2, NB], f32r)
    bd_hl = sb("bd_hl", [P, 2, 2, H], f32r)
    D1 = top[0]
    consts = sb("consts", [P, CONSTS], fp32)
    smalls = consts[:, 0:17]
    pat = consts[:, 17:C_FIRST].rearrange("p (f g) -> p f g", g=4)
    masks = consts[:, C_FIRST:C_FIRST + GT + P]
    ident = consts[:, C_FIRST + GT + P:C_FIRST + GT + 2 * P]
    iota_e = consts[:, C_FIRST + GT + 2 * P:CONSTS].rearrange("p (t e) -> p t e", e=E8)
    identb = sb("identb", [P, P], bf16)
    ints = sb("ints", [P, BATCH + 4 + TILES], i32)
    lang = ints[:, BATCH + 4:BATCH + 4 + TILES]
    ex_f = sb("ex_f", [P, BATCH + 4], fp32)
    ex_g = sb("ex_g", [P, BATCH + 4], fp32)
    ex_i = sb("ex_i", [P, BATCH], i32)
    idx_a = sb("idx_a", [P, BATCH], i32)
    idx_all = sb("idx_all", [P, FT, 4], i32)
    wm = sb("wm", [P, FT, 2], fp32)
    wdm = sb("wdm", [P, FT, 4], fp32)
    ws_all = sb("ws_all", [P, 2 * 2 * FT + 2 * 4], fp32)
    ws_t = sb("ws_t", [2 * 2 * FT + 8, P], fp32)
    ssq = sb("ssq", [P, TILES], fp32)
    qs = sb("qs", [P, 8, TILES], fp32)
    half = sb("half", [P, 1], fp32)
    warm = sb("warm", [P, 2], fp32)

    assert top[0] <= 229344, top[0]

    vu_raw = sb("vu_raw", [P, WCH, 2 * H], fp32, at=X0 + 4 * 2 * KT * NB)
    agu = sb("agu", [P, BATCH, 2 * KT * RANK], fp32, at=Y0)
    ag = [sb(f"ag{n}", [P, KT, KT, P], fp32, at=at) for n, at in enumerate((A0, Y0))]
    vr_raw = sb("vr_raw", [P, H], fp32, at=D0)
    vr_hl = sb("vr_hl", [P, H], f32r, at=D0 + 2048)
    c_hl = sb("c_hl", [P, H], f32r, at=D0 + 4096)
    ur = sb("ur", [4, H], fp32, at=D0 + 6144)
    bd_raw = sb("bd_raw", [P, 2, H], fp32, at=G0)
    nat = sb("nat", [P, 2, 3 * H], fp32, at=X0)
    x1_hl = sb("x1_hl", [P, 2, KT, T], f32r, at=X0)
    t_raw = [sb(f"t_raw{i}", [P, FP], fp32, at=at) for i, at in enumerate((W0, W0 + 4 * FP, D0 + 8704))]
    assert D0 + 8704 + 4 * FP <= D1
    at = W0 + 2 * FP * 4
    inv_b = sb("inv_b", [P, 2, F], fp32, at=at)
    ws_b = sb("ws_b", [P, 2, F], fp32, at=at + 8 * F)
    invd_b = sb("invd_b", [P, H], fp32, at=at + 16 * F)
    wsd_b = sb("wsd_b", [P, H], fp32, at=at + 16 * F + 2048)
    wq = sb("wq", [P, 2, KT, F], bf16, at=at + 16 * F + 4096)
    wqd_at = at + 16 * F + 4096 + 2 * KT * F * 2
    wqd = sb("wqd", [P, FT, H], bf16, at=wqd_at)
    assert wqd_at + FT * H * 2 <= W1
    wc_raw = sb("wc_raw", [P, KT, H], fp32, at=A1)
    bc_raw = sb("bc_raw", [P, H], fp32, at=wqd_at)
    wc_lo_hi = sb("wc_lo_hi", [P, 2, KT, H], f32r, at=A1)
    wc_hl = (wc_lo_hi[:, 1], wc_lo_hi[:, 0])
    awr = sb("awr", [P, KT, HT], fp32, at=A0)
    bc_hl = sb("bc_hl", [P, 2, H], f32r, at=A0 + 2176)
    rmsw = sb("rmsw", [P, H], fp32, at=A0 + 6272)
    h_sb = sb("h_sb", [P, TILES, HT], fp32, at=A0 + 8320)
    g_at = A0 + 12672
    lg = sb("lg", [P, TILES, E8], fp32, at=g_at)
    mx = sb("mx", [P, TILES, E8], fp32, at=g_at + 256)
    mi = sb("mi", [P, TILES, E8], u32, at=g_at + 512)
    oh = sb("oh", [P, 2, TILES, E8], fp32, at=g_at + 768)
    gates = sb("gates", [P, TILES, E8], fp32, at=g_at + 1280)
    gw = sb("gw", [P, 6, TILES], fp32, at=g_at + 1536)
    assert g_at + 1536 + 192 <= A1
    x1t = sb("x1t", [P, TILES, H], fp32, at=Y0)
    hgt_hl = sb("hgt_hl", [P, 2, T], f32r, at=Y0 + 16384)
    qt = sb("qt", [P, TILES, KT, P], bf16, at=Y0 + 24576)
    cw = sb("cw", [P, 3, H], fp32, at=D0)
    sq_junk = sb("sq_junk", [P, H], fp32, at=D0 + 6144)
    q1 = sb("q1", [P, 4, H], bf16, at=G0)
    g_sb = sb("g_sb", [P, 2, F], fp32, at=X0)
    u_sb = sb("u_sb", [P, 2, F], fp32, at=X0 + 8 * F)
    h_rnd = sb("h_rnd", [P, F], fp32, at=X0 + 16 * F)
    q2 = sb("q2", [P, 2, F], bf16, at=X0 + 20 * F)
    q2t = sb("q2t", [P, 2, FT, P], bf16, at=X0 + 24 * F)
    o_sb = sb("o_sb", [P, 2, H], fp32, at=X0 + 24 * F + 5632)
    r_sb = sb("r_sb", [P, 2, H], fp32, at=X0 + 24 * F + 9728)
    assert X0 + 24 * F + 9728 + 4096 <= W0

    s_at = {"sall": slice(0, 4), "alpha": slice(4, 5), "beta": slice(5, 6), "s_r": slice(6, 7),
            "d": slice(7, 8), "bias": slice(8, 12), "r": slice(12, 16)}

    def hf(t):
        return t.bitcast(fp32)

    with ExitStack() as ctx:
        def sem(name):
            return ctx.enter_context(nc.semaphore(name))

        ps = [ctx.enter_context(nc.psum_tensor(f"ps{i}", [P, NB], fp32)) for i in range(8)]
        psb = [p[:].bitcast(bf16) for p in ps]
        GATE, TD = 5, 4
        CB = (0, 1, 3, 2)
        UP = (6, 7)

        small_in, it_in, const_in, vr_in, ur_in, bd_in = map(sem, (
            "small_in", "it_in", "const_in", "vr_in", "ur_in", "bd_in"))
        x_in = [sem(f"x_in{i}") for i in range(3)]
        vu_in = [sem(f"vu_in{c}") for c in range(WCH)]
        u0_in = sem("u0_in")
        agu_in = [sem("agu_in0"), sem("agu_in1")]
        ad_in = [sem("ad_in0"), sem("ad_in1")]
        wg_in = [sem("wg_in0"), sem("wg_in1")]
        wd_in = [sem("wd_in0"), sem("wd_in1")]
        b_in = [sem("b_in0"), sem("b_in1")]
        nat_in = [sem("nat_in0"), sem("nat_in1")]
        t_in = [sem(f"t_in{i}") for i in range(3)]
        wc_in, bc_in, awr_in, rmsw_in, wsb_in, invb_in0 = map(sem, (
            "wc_in", "bc_in", "awr_in", "rmsw_in", "wsb_in", "invb_in0"))
        invb_in = [invb_in0, sem("invb_in1"), sem("invb_in2")]
        u_scaled, x_hi, x_lo, wg_hi, wg_lo, wd_hi, wd_lo, b_hi, b_lo, ad_hi, ad_lo, bd_hi, bd_lo = map(sem, (
            "u_scaled", "x_hi", "x_lo", "wg_hi", "wg_lo", "wd_hi", "wd_lo", "b_hi", "b_lo", "ad_hi", "ad_lo",
            "bd_hi", "bd_lo"))
        wg_used, down_done = sem("wg_used"), sem("down_done")
        idx_ready, vr_ready, urs_ready = map(sem, ("idx_ready", "vr_ready", "urs_ready"))
        cmix_ready, c_zero, c_hi, c_ready, we_ready, we_hi, we_lo = map(sem, (
            "cmix_ready", "c_zero", "c_hi", "c_ready", "we_ready", "we_hi", "we_lo"))
        tg_ready, tg_zero, tg_masked, tg_hi, tg_lo = map(sem, ("tg_ready", "tg_zero", "tg_masked", "tg_hi", "tg_lo"))
        gate_ready, silu_done, act_made, act_hi, act_lo = map(sem, (
            "gate_ready", "silu_done", "act_made", "act_hi", "act_lo"))
        td_masked, td_hi, td_lo, y_ready, y_hi, y_lo = map(sem, (
            "td_masked", "td_hi", "td_lo", "y_ready", "y_hi", "y_lo"))
        z_ready, x1_made, x1_hi, x1_lo = map(sem, ("z_ready", "x1_made", "x1_hi", "x1_lo"))
        nat_used, ws_made, wst_ready, wst_out, scr_out = map(sem, (
            "nat_used", "ws_made", "wst_ready", "wst_out", "scr_out"))
        t_scaled, t_quant = sem("t_scaled"), sem("t_quant")
        wc_hi, wc_lo, bc_hi, bc_lo = map(sem, ("wc_hi", "wc_lo", "bc_hi", "bc_lo"))
        h_ready, h_out, x1t_ready, x1t_out = map(sem, ("h_ready", "h_out", "x1t_ready", "x1t_out"))
        diff_made, exp_made, hg_made, hgt_ready, hgt_hi, hgt_lo = map(sem, (
            "diff_made", "exp_made", "hg_made", "hgt_ready", "hgt_hi", "hgt_lo"))
        cond_ready, cw_made, max_made, sq_made, rs_made, q1_scaled, q1_made, qt_ready, qt_out = map(sem, (
            "cond_ready", "cw_made", "max_made", "sq_made", "rs_made", "q1_scaled", "q1_made", "qt_ready", "qt_out"))
        gq_ready, uq_ready, g_made, u_made, sg_made, h_made, h_scaled, q2_made = map(sem, (
            "gq_ready", "uq_ready", "g_made", "u_made", "sg_made", "h_made", "h_scaled", "q2_made"))
        hq, q2t_ready, q2t_out, o_ready, o_made, r_made = map(sem, ("hq", "q2t_ready", "q2t_out", "o_ready", "o_made", "r_made"))
        out_done = [sem("out_done0"), sem("out_done1")]
        dve_step, pool_step, ag_made = sem("dve_step"), sem("pool_step"), sem("ag_made")
        u0_hi = sem("u0_hi")
        ms_made, s_step = sem("ms_made"), sem("s_step")
        last_q2t_out, last_made = sem("last_q2t_out"), sem("last_made")
        ident_b, warmed = sem("ident_b"), sem("warmed")

        block = ctx.enter_context(nc.Block())

        @block.sync
        def _(sp):
            sp.dma_start(ints[:], a["ints"]).then_inc(it_in, 16)
            sp.dma_start(consts[:, 0:C_FIRST], a["consts"][:, 0:C_FIRST]).then_inc(small_in, 16)

            def load_wg(s, slot, src):
                sp.wait_ge(wg_hi, WCH + s - 1)
                sp.wait_ge(wg_lo, WCH + s - 1)
                sp.dma_start(wg_raw[:, slot, :], src).then_inc(wg_in[slot], 16)

            def load_wd(s, slot, src):
                sp.wait_ge(wd_hi, s - 1)
                sp.wait_ge(wd_lo, s - 1)
                sp.dma_start(wd_raw[:, slot, :], src).then_inc(wd_in[slot], 16)

            def load_nat(s, slot, src):
                sp.wait_ge(nat_used, s - 1)
                sp.dma_start(nat[:, slot, :], src).then_inc(nat_in[slot], 16)

            def load_vu(c):
                sp.dma_start(vu_raw[:, c, :], a["w_vu"][c]).then_inc(vu_in[c], 16)

            load_vu(1)
            for i in range(2):
                k = slice(2 * i, 2 * i + 2)
                sp.dma_start(x_raw[:, k, 0:NB], a["x_t"][:, k, 0:NB]).then_inc(x_in[i], 16)
            sp.dma_start(wg_raw[:, 0, :], a["w_gu"][0]).then_inc(wg_in[0], 16)
            load_vu(2)
            sp.dma_start(consts[:, C_FIRST:CONSTS], a["consts"][:, C_FIRST:CONSTS]).then_inc(const_in, 16)
            load_vu(3)
            sp.dma_start(wg_raw[:, 1, :], a["w_gu"][1]).then_inc(wg_in[1], 16)
            for s in range(2):
                sp.dma_start(wd_raw[:, s, :], a["w_d"][s]).then_inc(wd_in[s], 16)
            sp.wait_ge(idx_ready, 1)
            with sp.Fori(0, HB) as b:
                e = sp.value_load(ex_i[0:1, ds(b, 1)], min_val=0, max_val=EXPERTS - 1)
                sp.dma_start(ad_raw[:, b, :], a["a_d"][e]).then_inc(ad_in[0], 16)
            sp.dma_start(x_raw[:, :, NB:T], a["x_t"][:, :, NB:T]).then_inc(x_in[2], 16)

            for n in range(NH):
                def step(f, par):
                    s, slot = n * FT + f, (n + par) % 2
                    load_wg(s, slot, a["w_gu"][f])
                    load_wd(s, slot, a["w_d"][f])
                    if n == 1:
                        load_nat(f, par, a["w_nat"][f])

                if n == 1:
                    for f in range(2):
                        s, slot = n * FT + f, (n + f) % 2
                        load_wg(s, slot, a["w_gu"][f])
                        load_wd(s, slot, a["w_d"][f])
                    sp.wait_ge(wg_used, WCH + FT)
                    for f in range(2):
                        sp.dma_start(nat[:, f, :], a["w_nat"][f]).then_inc(nat_in[f], 16)
                step(2, 0)
                if n == 1:
                    sp.dma_start(wc_raw[:], a["wc_t"]).then_inc(wc_in, 16)
                    sp.wait_ge(ad_hi, FT)
                    sp.wait_ge(ad_lo, FT)
                    for k in range(2):
                        sp.dma_start(t_raw[k][:, 0:F], a["wg_t"][k]).then_inc(t_in[k], 16)
                with sp.Fori(0, (FT - 3) // 2) as j:
                    step(2 * j + 3, 1)
                    step(2 * j + 4, 0)

            sp.wait_ge(wst_out, 1)
            sp.dma_start(scratch, ws_t[:]).then_inc(scr_out, 16)
            sp.wait_ge(wg_used, WCH + STEPS)
            sp.wait_ge(down_done, STEPS)
            sp.dma_start(awr[:], a["awr"]).then_inc(awr_in, 16)
            sp.wait_ge(scr_out, 16)
            sp.wait_ge(ad_hi, STEPS)
            sp.wait_ge(ad_lo, STEPS)
            for gu in range(2):
                r = 2 * FT + gu * FT
                sp.dma_start(inv_b[:, gu, :], scratch[r:r + FT, :].rearrange("(o f) p -> o (f p)", o=1)[:, 0:F]
                             .broadcast_to([P, F])).then_inc(invb_in[gu], 16)
            sp.dma_start(bc_raw[:], a["bc"]).then_inc(bc_in, 16)

            def load_t(c):
                if c < 8:
                    dst, src = t_raw[c % 3][:, 0:F], a["wg_t" if c < 4 else "wu_t"][c % 4]
                else:
                    f, w = 2 * (c - 8), min(2, FT - 2 * (c - 8))
                    dst = t_raw[c % 3][:, 0:w * H].rearrange("p (w h) -> p w h", w=w)
                    src = a["wd_t"][:, f:f + w, :]
                sp.dma_start(dst, src).then_inc(t_in[c % 3], 16)

            sp.wait_ge(y_ready, 2 * KT)
            load_t(2)
            sp.dma_start(rmsw[:], a["rmsw"]).then_inc(rmsw_in, 16)
            for c in range(3, 14):
                sp.wait_ge(t_quant, c - 2)
                load_t(c)
                if c == 5:
                    sp.dma_start(invd_b[:], scratch[4 * FT + 4:4 * FT + 8, :].rearrange("(o f) p -> o (f p)", o=1)
                                 .broadcast_to([P, H])).then_inc(invb_in[2], 16)
            for gu in range(2):
                r = gu * FT
                sp.dma_start(ws_b[:, gu, :], scratch[r:r + FT, :].rearrange("(o f) p -> o (f p)", o=1)[:, 0:F]
                             .broadcast_to([P, F])).then_inc(wsb_in, 16)
            sp.dma_start(wsd_b[:], scratch[4 * FT:4 * FT + 4, :].rearrange("(o f) p -> o (f p)", o=1)
                         .broadcast_to([P, H])).then_inc(wsb_in, 16)

            def store(t, slot):
                sp.wait_ge(r_made, t + 1)
                sp.dma_start(out[t], r_sb[:, slot, :]).then_inc(out_done[slot], 16)

            with sp.Fori(0, TILES // 2 - 1) as j:
                store(2 * j, 0)
                store(2 * j + 1, 1)
            store(TILES - 2, 0)
            for i in range(2):
                cols = slice(i * HH, (i + 1) * HH)
                sp.wait_ge(last_made, i + 1)
                sp.dma_start(out[TILES - 1][:, cols], r_sb[:, 1, cols]).then_inc(out_done[1], 16)
            sp.wait_ge(out_done[0], 16 * TILES // 2)
            sp.wait_ge(out_done[1], 16 * (TILES // 2 + 1))

        @block.gpsimd
        def _(gp):
            nc.gpsimd.memset(half[:], -0.5).then_inc(pool_step, 1)
            gp.wait_ge(pool_step, 1)

            def gather_a(table, tile, b, done):
                gp.indirect_dma_start(
                    out=tile[:, b, :], out_offset=None, in_=a[table].rearrange("e p c -> (e p) c"),
                    in_offset=bass.IndirectOffsetOnAxis(ap=idx_a[:, b:b + 1], axis=0),
                ).then_inc(done, 16)

            def gather_b(s):
                n, f = divmod(s, FT)
                slot = s % 2
                if s >= 2:
                    gp.wait_ge(b_hi, s - 1)
                    gp.wait_ge(b_lo, s - 1)
                for g in range(2):
                    gp.indirect_dma_start(
                        out=b_raw[:, slot, g, :], out_offset=None, in_=a["b_gu"],
                        in_offset=bass.IndirectOffsetOnAxis(ap=idx_all[:, f, 2 * n + g:2 * n + g + 1], axis=0),
                    ).then_inc(b_in[slot], 16)

            def gather_bd(n):
                if n == 0:
                    gp.wait_ge(tg_hi, NH)
                    gp.wait_ge(tg_lo, NH)
                else:
                    gp.wait_ge(bd_hi, n)
                    gp.wait_ge(bd_lo, n)
                for g in range(2):
                    gp.indirect_dma_start(
                        out=bd_raw[:, g, :], out_offset=None, in_=a["b_d"],
                        in_offset=bass.IndirectOffsetOnAxis(ap=idx_all[:, 0, 2 * n + g:2 * n + g + 1], axis=0),
                    ).then_inc(bd_in, 16)

            gp.wait_ge(idx_ready, 1)
            for b in range(HB):
                gather_a("a_gu", agu, b, agu_in[0])
            for s in range(STEPS):
                gather_b(s)
                if 2 <= s < 6:
                    for b in range(4 * s - 8, 4 * s - 4):
                        gather_a("a_gu", agu, HB + b, agu_in[1])
                if 6 <= s < 10:
                    for b in range(4 * s - 24, 4 * s - 20):
                        gather_a("a_d", ad_raw, HB + b, ad_in[1])
                if s == FT + 1:
                    gather_bd(0)
            gather_bd(1)

            def rms_scale(t):
                gp.wait_ge(ms_made, t + 1)
                nc.gpsimd.tensor_tensor(qs[:, 2, t:t + 1], qs[:, 0, t:t + 1], half[:], ALU.pow).then_inc(rs_made, 1)

            for c in range(14):
                if c >= 8:
                    rms_scale(c - 8)
                gp.wait_ge(t_in[c % 3], 16 * (c // 3 + 1))
                gp.wait_ge(invb_in[0 if c < 4 else 1 if c < 8 else 2], 16)
                if c < 8:
                    src, by = t_raw[c % 3][:, 0:F], inv_b[:, c // 4, :]
                else:
                    w = min(2, FT - 2 * (c - 8))
                    src = t_raw[c % 3][:, 0:w * H].rearrange("p (w h) -> p w h", w=w)
                    by = invd_b[:].unsqueeze(1).broadcast_to([P, w, H])
                nc.gpsimd.tensor_tensor(src, src, by, ALU.mult).then_inc(t_scaled, 1)

            for t in range(14 - 8, TILES):
                rms_scale(t)

            def h_mul(t, slot):
                for c in range(3):
                    cols = slice(CO[c], CO[c] + CH[c])
                    gp.wait_ge(sg_made, 3 * t + c + 1)
                    gp.wait_ge(u_made, 3 * t + c + 1)
                    nc.gpsimd.tensor_tensor(g_sb[:, slot, cols], g_sb[:, slot, cols], u_sb[:, slot, cols],
                                            ALU.mult).then_inc(h_made, 1)

            def residual(t, slot):
                gp.wait_ge(o_made, t + 1)
                gp.wait_ge(x1t_out, TILES)
                if not (isinstance(t, int) and t < 2):
                    gp.wait_ge(out_done[slot], 8 * (t - slot))
                nc.gpsimd.tensor_tensor(r_sb[:, slot, :], o_sb[:, slot, :], x1t[:, t, :], ALU.add).then_inc(r_made, 1)

            for t in range(2):
                h_mul(t, t)
            for t in (2, 3):
                h_mul(t, t % 2)
                residual(t - 2, t % 2)
            with gp.Fori(0, TILES // 2 - 2) as j:
                for d in range(2):
                    h_mul(2 * j + 4 + d, d)
                    residual(2 * j + 2 + d, d)
            residual(TILES - 2, 0)

        @block.scalar
        def _(act):
            def copy(o, i):
                return nc.scalar.activation(o, i, ACT.Copy)

            act.dma_start(vu_raw[:, 0, H:2 * H], a["w_vu"][0][:, H:2 * H]).then_inc(u0_in, 16)
            act.dma_start(vu_raw[:, 0, 0:H], a["w_vu"][0][:, 0:H]).then_inc(vu_in[0], 16)
            act.dma_start(ur[:], a["ur"]).then_inc(ur_in, 16)
            act.dma_start(vr_raw[:], a["vr"]).then_inc(vr_in, 16)
            act.wait_ge(pool_step, 1)
            nc.scalar.activation(warm[:, 0:1], half[:], ACT.Silu).then_inc(warmed, 1)

            def vu_split(c):
                act.wait_ge(vu_in[c], 16)
                act.wait_ge(u_scaled, c + 1)
                if c == 2:
                    act.wait_ge(wg_used, 2)
                if c == 3:
                    act.wait_ge(wg_used, 3)
                copy(wg_hl[:, VU_SLOT[c], HI, :], vu_raw[:, c, :]).then_inc(wg_hi, 1)

            def wg_split(s, slot):
                act.wait_ge(wg_in[slot], 8 * (s - slot) + 16)
                act.wait_ge(wg_used, {0: 1, 1: 3}[s] if isinstance(s, int) and s < 2 else WCH + s - 1)
                copy(wg_hl[:, slot, HI, :], wg_raw[:, slot, :]).then_inc(wg_hi, 1)

            def b_split(s, slot):
                act.wait_ge(b_in[slot], 16 * (s - slot) + 32)
                copy(b_hl[:, slot, HI, :, :], b_raw[:, slot, :, :]).then_inc(b_hi, 1)

            def ad_split(s, slot, f, n):
                copy(ad_hl[:, slot, HI, :].rearrange("p (b r) -> p b r", b=HB),
                     ad_raw[:, n * HB:(n + 1) * HB, ds(f * RANK, RANK)]).then_inc(ad_hi, 1)

            def wd_split(s, slot):
                act.wait_ge(wd_in[slot], 8 * (s - slot) + 16)
                copy(wd_hl[:, slot, HI, :], wd_raw[:, slot, :]).then_inc(wd_hi, 1)

            act.wait_ge(u_scaled, 1)
            copy(wg_hl[:, 0, HI, H:2 * H], vu_raw[:, 0, H:2 * H]).then_inc(u0_hi, 1)
            act.wait_ge(vu_in[0], 16)
            copy(wg_hl[:, 0, HI, 0:H], vu_raw[:, 0, 0:H]).then_inc(wg_hi, 1)
            vu_split(1)
            act.wait_ge(vr_in, 16)
            copy(vr_hl[:], vr_raw[:]).then_inc(vr_ready, 1)
            for i in range(2):
                act.wait_ge(x_in[i], 16)
                copy(x_hl[0][:, HI, 2 * i:2 * i + 2], x_raw[:, 2 * i:2 * i + 2, 0:NB]).then_inc(x_hi, 1)
            wg_split(0, 0)
            act.wait_ge(cmix_ready, 1)
            act.wait_ge(c_zero, 1)
            copy(c_hl[0:4, :], ps[TD][0:4, :]).then_inc(c_hi, 1)
            copy(c_hl[64:68, :], ps[TD][0:4, :]).then_inc(c_hi, 1)
            vu_split(2)
            vu_split(3)
            b_split(0, 0)
            wg_split(1, 1)

            def tg_split(n):
                act.wait_ge(tg_masked, 4 * (n + 1))
                copy(tg_hl[:, n, HI], tg_tmp[:]).then_inc(tg_hi, 1)

            tg_split(0)
            b_split(1, 1)

            def silu(s):
                act.wait_ge(gate_ready, s + 1)
                if not (isinstance(s, int) and s < 1):
                    act.wait_ge(act_made, s)
                nc.scalar.activation(sil[:], ps[GATE][:], ACT.Silu).then_inc(silu_done, 1)

            def act_split(s, slot):
                act.wait_ge(act_made, s + 1)
                if not (isinstance(s, int) and s < 2):
                    act.wait_ge(down_done, s - 1)
                copy(act_hl[:, slot, HI, :], act_raw[:]).then_inc(act_hi, 1)

            def step(f, par, n, split_next=True, gate=True):
                s, slot = n * FT + f, (n + par) % 2
                if split_next:
                    wg_split(s + 1, 1 - slot)
                    b_split(s + 1, 1 - slot)
                if gate:
                    silu(s)
                if not (isinstance(s, int) and s < 2):
                    act.wait_ge(down_done, s - 1)
                ad_split(s, slot, f, n)
                wd_split(s, slot)
                act_split(s, slot)

            def bd_split(n):
                act.wait_ge(bd_in, 32 * (n + 1))
                if n:
                    act.wait_ge(y_ready, KT * n)
                copy(bd_hl[:, HI], bd_raw[:]).then_inc(bd_hi, 1)

            def y_out(n):
                for m in range(KT):
                    act.wait_ge(y_ready, KT * n + m + 1)
                    copy(y_hl[:, HI, m, :], ps[m][:]).then_inc(y_hi, 1)

            silu(0)
            for i in range(KT):
                act.wait_ge(we_ready, i + 1)
                copy(we_hl[:, HI, i, :], ps[i][:]).then_inc(we_hi, 1)
            act.wait_ge(ad_in[0], 16 * HB)
            step(0, 0, 0, split_next=False, gate=False)
            step(1, 1, 0)
            act.wait_ge(wg_lo, WCH)
            act.wait_ge(x_in[2], 16)
            copy(x_hl[1][:, HI], x_raw[:, :, NB:T]).then_inc(x_hi, 1)
            step(2, 0, 0)
            with act.Fori(0, (FT - 3) // 2) as j:
                step(2 * j + 3, 1, 0)
                step(2 * j + 4, 0, 0)
            tg_split(1)
            act.wait_ge(ad_in[1], 16 * HB)
            step(0, 0, 1)
            act.wait_ge(td_masked, 1)
            copy(td_hl[:, HI], td_raw[:]).then_inc(td_hi, 1)
            bd_split(0)
            step(1, 1, 1)
            y_out(0)
            step(2, 0, 1)
            with act.Fori(0, (FT - 5) // 2) as j:
                step(2 * j + 3, 1, 1)
                step(2 * j + 4, 0, 1)
            step(FT - 2, 1, 1)
            step(FT - 1, 0, 1, split_next=False)

            def x1_split(q):
                n, m = divmod(q, KT)
                act.wait_ge(x1_made, q + 1)
                copy(x1_hl[:, HI, m, n * NB:(n + 1) * NB], x_raw[:, m, n * NB:(n + 1) * NB]).then_inc(x1_hi, 1)

            act.wait_ge(wc_in, 16)
            act.wait_ge(wg_used, WCH + STEPS)
            copy(wc_hl[HI], wc_raw[:]).then_inc(wc_hi, 1)
            x1_split(0)
            act.wait_ge(wst_ready, 1)
            copy(ws_t[:], ps[7][0:2 * 2 * FT + 8, 0:P]).then_inc(wst_out, 1)
            x1_split(1)
            act.wait_ge(td_masked, 2)
            copy(td_hl[:, HI], td_raw[:]).then_inc(td_hi, 1)
            bd_split(1)
            x1_split(2)
            x1_split(3)
            y_out(1)
            def h_copy(i):
                bank, t0, nt = ((4, 0, 3), (3, 3, 3), (4, 6, 2))[i]
                act.wait_ge(h_ready, t0 + nt)
                copy(h_sb[:, t0:t0 + nt, :], ps[bank][:, 0:nt * HT].rearrange("p (t h) -> p t h", t=nt)).then_inc(h_out, 1)

            h_copy(0)

            def x1t_copy(t):
                act.wait_ge(x1t_ready, t + 1)
                copy(x1t[:, t, :], ps[(5, 6, 7)[t % 3]][:]).then_inc(x1t_out, 1)

            x1_split(4)
            act.wait_ge(bc_in, 16)
            copy(bc_hl[:, HI], bc_raw[:]).then_inc(bc_hi, 1)
            x1_split(5)
            x1_split(6)
            x1t_copy(0)
            x1t_copy(1)
            x1_split(7)
            x1t_copy(2)
            x1t_copy(3)
            h_copy(1)
            h_copy(2)
            nc.scalar.activation(warm[:, 1:2], half[:], ACT.Exp).then_inc(warmed, 1)
            x1t_copy(4)
            x1t_copy(5)
            act.wait_ge(diff_made, 1)
            nc.scalar.activation(gw[:, 1, :], gw[:, 0, :], ACT.Exp).then_inc(exp_made, 1)
            x1t_copy(6)
            x1t_copy(7)
            act.wait_ge(warmed, 2)
            nc.scalar.activation(warm[:, 1:2], half[:], ACT.Silu).then_inc(warmed, 1)
            for i in range(2):
                act.wait_ge(hgt_ready, i + 1)
                copy(hgt_hl[:, HI, i * NB:(i + 1) * NB], ps[5 + i][:]).then_inc(hgt_hi, 1)

            def q1_round(t):
                act.wait_ge(q1_scaled, t + 1)
                if t >= 4:
                    act.wait_ge(qt_ready, t - 3)
                nc.scalar.activation(q1[:, t % 4, :], cw[:, t % 3, :], ACT.Copy, bias=-ROUND).then_inc(q1_made, 1)

            def qt_copy(t):
                act.wait_ge(qt_ready, t + 1)
                copy(qt[:, t, :, :].rearrange("p k m -> p (k m)"), psb[(7, 6)[t % 2]][:, 0:H]).then_inc(qt_out, 1)

            for t in range(TILES):
                act.wait_ge(cond_ready, t + 1)
                if t:
                    act.wait_ge(sq_made, t)
                nc.scalar.activation(sq_junk[:], ps[CB[t % 4]][:], ACT.Square, accum_out=ssq[:, t:t + 1]).then_inc(sq_made, 1)
                if t >= 4:
                    qt_copy(t - 4)
                if t >= 2:
                    q1_round(t - 2)
            q1_round(TILES - 2)
            qt_copy(TILES - 4)
            q1_round(TILES - 1)
            for t in range(TILES - 3, TILES):
                qt_copy(t)

            def l1_silu(t, slot, c):
                part = g_sb[:, slot, CO[c]:CO[c] + CH[c]]
                act.wait_ge(g_made, 3 * t + c + 1)
                nc.scalar.activation(part, part, ACT.Silu).then_inc(sg_made, 1)

            def q2_round(t, slot):
                if not (isinstance(t, int) and t < 2):
                    act.wait_ge(q2t_ready, 2 * t - 2)
                for i, cols in enumerate(Q2_PARTS):
                    act.wait_ge(h_scaled, 2 * t + i + 1)
                    nc.scalar.activation(q2[:, slot, cols], h_rnd[:, cols], ACT.Copy, bias=-ROUND).then_inc(q2_made, 1)

            def q2t_copy(t, slot, part, bank=6):
                act.wait_ge(q2t_ready, 2 * t + part + 1)
                if part == 0:
                    if not (isinstance(t, int) and t < 2):
                        act.wait_ge(o_ready, t - 1)
                    copy(q2t[:, slot, 0:6, :], psb[bank][:, 0:6 * P].rearrange("p (j m) -> p j m", j=6)).then_inc(q2t_out, 1)
                else:
                    copy(q2t[:, slot, 6:10, :], psb[bank][:, 0:4 * P].rearrange("p (j m) -> p j m", j=4))
                    copy(q2t[0:FREM, slot, 10, :], psb[bank][0:FREM, 4 * P:5 * P]).then_inc(q2t_out, 1)

            def l1_step(t, slot):
                l1_silu(t, slot, 0)
                q2t_copy(t - 2, slot, 0)
                l1_silu(t, slot, 1)
                q2t_copy(t - 2, slot, 1)
                q2_round(t - 1, 1 - slot)
                l1_silu(t, slot, 2)

            for t in range(2):
                for c in range(3):
                    l1_silu(t, t, c)
            q2_round(0, 0)
            for t in (2, 3):
                l1_step(t, t % 2)
            with act.Fori(0, TILES // 2 - 2) as j:
                for d in range(2):
                    l1_step(2 * j + 4 + d, d)
            q2t_copy(TILES - 2, 0, 0)
            q2t_copy(TILES - 2, 0, 1, bank=0)
            q2_round(TILES - 1, 1)
            q2t_copy(TILES - 1, 1, 0)

        @block.vector
        def _(dve):
            steps = [0]

            def link(ins):
                steps[0] += 1
                ins.then_inc(dve_step, 1)
                dve.wait_ge(dve_step, steps[0])

            V = nc.vector
            dve.wait_ge(it_in, 16)
            link(V.tensor_copy(ex_f[:], ints[:, 0:BATCH + 4]))
            link(V.tensor_scalar(ex_g[:], ex_f[:], 0.0, float(EXPERTS), ALU.is_lt, ALU.mult))
            link(V.tensor_tensor(ex_f[:], ex_f[:], ex_g[:], ALU.add))
            link(V.tensor_scalar(ex_f[:], ex_f[:], 0.0, float(EXPERTS - 1), ALU.max, ALU.min))
            V.tensor_copy(ex_i[:], ex_f[:, 0:BATCH])
            dve.wait_ge(small_in, 16)
            V.tensor_scalar(idx_a[:], ex_f[:, 0:BATCH], float(P), smalls[:, 16:17], ALU.mult, ALU.add)
            link(V.scalar_tensor_tensor(idx_all[:], ex_f[:, BATCH:BATCH + 4].unsqueeze(1).broadcast_to([P, FT, 4]),
                                        float(RANK), pat, ALU.mult, ALU.add))
            V.memset(ssq[:], 0.0).then_inc(idx_ready, 1)
            link(V.tensor_scalar(smalls[0:64, 0:1], smalls[0:64, 0:1], smalls[0:64, s_at["alpha"]],
                                 smalls[0:64, s_at["beta"]], ALU.mult, ALU.add))
            link(V.tensor_scalar(smalls[0:64, 0:1], smalls[0:64, 0:1], 0.0, None, ALU.max))
            link(V.tensor_scalar(smalls[0:4, s_at["d"]], smalls[0:4, s_at["d"]], 0.0, smalls[0:4, s_at["s_r"]],
                                 ALU.max, ALU.mult))

            def lo(o, raw, hi):
                return V.tensor_tensor(o, raw, hf(hi), ALU.subtract)

            def u_scale(c):
                dve.wait_ge(u0_in if c == 0 else vu_in[c], 16)
                V.tensor_scalar(vu_raw[:, c, H:2 * H], vu_raw[:, c, H:2 * H], smalls[:, c:c + 1], None,
                                ALU.mult).then_inc(u_scaled, 1)

            def vu_split(c):
                slot = VU_SLOT[c]
                dve.wait_ge(wg_hi, VU_TURN[c])
                lo(wg_hl[:, slot, LO, :], vu_raw[:, c, :], wg_hl[:, slot, HI, :]).then_inc(wg_lo, 1)

            def wg_split(s, slot):
                dve.wait_ge(wg_in[slot], 8 * (s - slot) + 16)
                dve.wait_ge(wg_hi, STEP0_TURN if isinstance(s, int) and s < 1 else WCH + s + 1)
                lo(wg_hl[:, slot, LO, :], wg_raw[:, slot, :], wg_hl[:, slot, HI, :]).then_inc(wg_lo, 1)

            def b_split(s, slot):
                dve.wait_ge(b_hi, s + 1)
                lo(b_hl[:, slot, LO, :, :], b_raw[:, slot, :, :], b_hl[:, slot, HI, :, :]).then_inc(b_lo, 1)

            def ag_copy(n):
                dve.wait_ge(agu_in[n], 16 * HB)
                for j in range(KT):
                    b = n * HB + 4 * j
                    V.tensor_copy(ag[n][:, j].rearrange("p k (g b r) -> p (k g) b r", g=2, b=4),
                                  agu[:, b:b + 4, :].rearrange("p b (q r) -> p q b r", r=RANK)).then_inc(ag_made, 1)

            u_scale(0)
            dve.wait_ge(u0_hi, 1)
            lo(wg_hl[:, 0, LO, H:2 * H], vu_raw[:, 0, H:2 * H], wg_hl[:, 0, HI, H:2 * H])
            dve.wait_ge(wg_hi, 1)
            lo(wg_hl[:, 0, LO, 0:H], vu_raw[:, 0, 0:H], wg_hl[:, 0, HI, 0:H]).then_inc(wg_lo, 1)
            u_scale(1)
            vu_split(1)
            dve.wait_ge(ur_in, 16)
            V.tensor_scalar(ur[:], ur[:], smalls[0:4, s_at["d"]], None, ALU.mult).then_inc(urs_ready, 1)
            for i in range(2):
                k = slice(2 * i, 2 * i + 2)
                dve.wait_ge(x_hi, i + 1)
                lo(x_hl[0][:, LO, k], x_raw[:, k, 0:NB], x_hl[0][:, HI, k]).then_inc(x_lo, 1)
            wg_split(0, 0)
            V.memset(c_hl[:].bitcast(u32), 0).then_inc(c_zero, 1)
            V.memset(tg_tmp[:], 0.0).then_inc(tg_zero, 1)
            dve.wait_ge(vr_ready, 1)
            lo(vr_hl[64:P, :], vr_raw[64:P, :], vr_hl[64:P, :]).then_inc(vr_ready, 1)
            dve.wait_ge(c_hi, 2)
            dve.wait_ge(cmix_ready, 1)
            V.tensor_tensor(c_hl[32:36, :], ps[TD][0:4, :], hf(c_hl[0:4, :]), ALU.subtract).then_inc(c_ready, 1)
            V.tensor_tensor(c_hl[96:100, :], ps[TD][0:4, :], hf(c_hl[0:4, :]), ALU.subtract).then_inc(c_ready, 1)
            u_scale(2)
            vu_split(2)
            ag_copy(0)
            u_scale(3)
            vu_split(3)
            dve.wait_ge(const_in, 16)
            V.tensor_copy(identb[:], ident).then_inc(ident_b, 1)
            b_split(0, 0)

            def tg_split(n):
                dve.wait_ge(tg_zero, 1)
                dve.wait_ge(tg_ready, n + 1)
                if n:
                    dve.wait_ge(tg_hi, n)
                    dve.wait_ge(tg_lo, n)
                for gu in range(2):
                    for par in range(2):
                        rows = slice(64 * gu, 64 * gu + 64)
                        V.tensor_tensor(
                            tg_tmp[64 * par:64 * par + 64, gu, :].rearrange("p (g t) -> p g t", t=P)[:, par::2, :],
                            ps[UP[1]][rows, :].rearrange("p (g t) -> p g t", t=P)[:, par::2, :],
                            masks[rows, GT:GT + P].unsqueeze(1).broadcast_to([64, 2, P]), ALU.mult).then_inc(tg_masked, 1)
                if n == 0:
                    wg_split(1, 1)
                dve.wait_ge(tg_masked, 4 * (n + 1))
                dve.wait_ge(tg_hi, n + 1)
                lo(tg_hl[:, n, LO], tg_tmp[:], tg_hl[:, n, HI]).then_inc(tg_lo, 1)

            tg_split(0)
            b_split(1, 1)
            for i in range(KT):
                dve.wait_ge(we_hi, i + 1)
                lo(we_hl[:, LO, i, :], ps[i][:], we_hl[:, HI, i, :]).then_inc(we_lo, 1)

            def make_act(s, par):
                dve.wait_ge(silu_done, s + 1)
                dve.wait_ge(wg_used, WCH + s + 1)
                if not (isinstance(s, int) and s < 1):
                    dve.wait_ge(act_lo, s)
                V.tensor_tensor(act_raw[:], ps[UP[par]][:], sil[:], ALU.mult).then_inc(act_made, 1)

            def nat_max(f, par):
                dve.wait_ge(nat_in[par], 8 * (f - par) + 16)
                V.tensor_reduce(wm[:, f, :],
                                nat[:, par, 0:2 * H].rearrange("p (g h) -> p g h", g=2), X, ALU.max,
                                apply_absolute_value=True)
                V.tensor_reduce(wdm[:, f, :],
                                nat[:, par, 2 * H:3 * H].rearrange("p (g h) -> p g h", g=4), X, ALU.max,
                                apply_absolute_value=True).then_inc(nat_used, 1)

            def step(f, par, n, split_next=True, take_max=True):
                s, slot = n * FT + f, (n + par) % 2
                if split_next:
                    wg_split(s + 1, 1 - slot)
                    b_split(s + 1, 1 - slot)
                make_act(s, slot)
                dve.wait_ge(ad_hi, s + 1)
                lo(ad_hl[:, slot, LO, :].rearrange("p (b r) -> p b r", b=HB),
                   ad_raw[:, n * HB:(n + 1) * HB, ds(f * RANK, RANK)],
                   ad_hl[:, slot, HI, :].rearrange("p (b r) -> p b r", b=HB)).then_inc(ad_lo, 1)
                dve.wait_ge(wd_hi, s + 1)
                lo(wd_hl[:, slot, LO, :], wd_raw[:, slot, :], wd_hl[:, slot, HI, :]).then_inc(wd_lo, 1)
                dve.wait_ge(act_hi, s + 1)
                lo(act_hl[:, slot, LO, :], act_raw[:], act_hl[:, slot, HI, :]).then_inc(act_lo, 1)
                if n == 1 and take_max:
                    nat_max(f, par)

            def td_mask(n):
                dve.wait_ge(down_done, FT * (n + 1))
                if n:
                    dve.wait_ge(td_lo, n)
                V.tensor_tensor(td_raw[:].rearrange("p (g t) -> p g t", g=2),
                                ps[TD][:].rearrange("p (g t) -> p g t", g=2),
                                masks[:, 0:GT].unsqueeze(1).broadcast_to([P, 2, GT]), ALU.mult).then_inc(td_masked, 1)
                dve.wait_ge(td_hi, n + 1)
                lo(td_hl[:, LO], td_raw[:], td_hl[:, HI]).then_inc(td_lo, 1)
                dve.wait_ge(bd_hi, n + 1)
                lo(bd_hl[:, LO], bd_raw[:], bd_hl[:, HI]).then_inc(bd_lo, 1)

            def y_out(n):
                for m in range(KT):
                    dve.wait_ge(y_hi, KT * n + m + 1)
                    lo(y_hl[:, LO, m, :], ps[m][:], y_hl[:, HI, m, :]).then_inc(y_lo, 1)

            step(0, 0, 0, split_next=False)
            step(1, 1, 0)
            dve.wait_ge(x_hi, 3)
            lo(x_hl[1][:, LO], x_raw[:, :, NB:T], x_hl[1][:, HI]).then_inc(x_lo, 1)
            step(2, 0, 0)
            with dve.Fori(0, (FT - 5) // 2) as j:
                step(2 * j + 3, 1, 0)
                step(2 * j + 4, 0, 0)
            ag_copy(1)
            step(FT - 2, 1, 0)
            step(FT - 1, 0, 0)
            tg_split(1)
            step(0, 0, 1)
            td_mask(0)
            step(1, 1, 1, take_max=False)
            y_out(0)
            nat_max(1, 1)
            step(2, 0, 1)
            with dve.Fori(0, (FT - 5) // 2) as j:
                step(2 * j + 3, 1, 1)
                step(2 * j + 4, 0, 1)
            step(FT - 2, 1, 1)
            step(FT - 1, 0, 1, split_next=False)

            ZB = (5, 6, 7, 5, 5, 0, 1, 2)

            def x1_out(q):
                n, m = divmod(q, KT)
                here = x_raw[:, m, n * NB:(n + 1) * NB]
                dve.wait_ge(z_ready, q + 1)
                V.scalar_tensor_tensor(here, ps[ZB[q]][:], smalls[:, 8 + m:9 + m], here, ALU.add,
                                       ALU.add).then_inc(x1_made, 1)
                dve.wait_ge(x1_hi, q + 1)
                lo(x1_hl[:, LO, m, n * NB:(n + 1) * NB], here, x1_hl[:, HI, m, n * NB:(n + 1) * NB]).then_inc(x1_lo, 1)

            dve.wait_ge(nat_used, FT)
            NG = 2 * FT
            link(V.tensor_copy(ws_all[:, 0:NG].rearrange("p (g f) -> p g f", g=2), wm[:].rearrange("p f g -> p g f")))
            link(V.tensor_reduce(ws_all[:, 2 * NG:2 * NG + 4], wdm[:].rearrange("p f m -> p m f"), X, ALU.max))
            for o in (0, 2 * NG):
                w = NG if o == 0 else 4
                link(V.tensor_scalar(ws_all[:, o:o + w], ws_all[:, o:o + w], 1.0 / QMAX, Q_GUARD, ALU.mult, ALU.max))
                last = V.reciprocal(ws_all[:, o + w:o + 2 * w], ws_all[:, o:o + w])
                if o == 0:
                    link(last)
                else:
                    last.then_inc(ws_made, 1)
            dve.wait_ge(wc_hi, 1)
            lo(wc_hl[LO], wc_raw[:], wc_hl[HI]).then_inc(wc_lo, 1)
            x1_out(0)
            x1_out(1)
            td_mask(1)
            x1_out(2)
            x1_out(3)
            y_out(1)
            def t_round(c):
                dve.wait_ge(t_scaled, c + 1)
                if c < 8:
                    src, dst = t_raw[c % 3][:, 0:F], wq[:, c // 4, c % 4, :]
                else:
                    f, w = 2 * (c - 8), min(2, FT - 2 * (c - 8))
                    src = t_raw[c % 3][:, 0:w * H].rearrange("p (w h) -> p w h", w=w)
                    dst = wqd[:, f:f + w, :]
                V.tensor_scalar(dst, src, ROUND, ROUND, ALU.add, ALU.subtract).then_inc(t_quant, 1)

            x1_out(4)
            dve.wait_ge(bc_hi, 1)
            lo(bc_hl[:, LO], bc_raw[:], bc_hl[:, HI]).then_inc(bc_lo, 1)
            t_round(0)
            x1_out(5)
            t_round(1)
            x1_out(6)
            x1_out(7)
            t_round(2)
            t_round(3)

            L3 = [P, TILES, E8]
            link(V.tensor_tensor(oh[:, 0], iota_e, lang.unsqueeze(2).broadcast_to(L3), ALU.is_equal))
            t_round(4)
            dve.wait_ge(h_out, 3)
            link(V.scalar_tensor_tensor(lg[:], oh[:, 0], LANG_BIAS, h_sb[:, :, E8 * R8:HT], ALU.mult, ALU.add))
            for t in range(TILES):
                last = V.max(mx[:, t, :], lg[:, t, :])
            link(last)
            for t in range(TILES):
                last = V.max_index(mi[:, t, :], mx[:, t, :], lg[:, t, :])
            link(last)
            V.tensor_tensor(gw[:, 0, :], mx[:, :, 1], mx[:, :, 0], ALU.subtract).then_inc(diff_made, 1)
            for k in range(2):
                last = V.tensor_tensor(oh[:, k], iota_e, mi[:, :, k:k + 1].broadcast_to(L3), ALU.is_equal)
            link(last)
            dve.wait_ge(exp_made, 1)
            link(V.tensor_scalar(gw[:, 2, :], gw[:, 1, :], 1.0, None, ALU.add))
            link(V.reciprocal(gw[:, 3, :], gw[:, 2, :]))
            link(V.tensor_scalar(gw[:, 4, :], gw[:, 3, :], MOE_SCALE, None, ALU.mult))
            link(V.tensor_tensor(gw[:, 5, :], gw[:, 4, :], gw[:, 1, :], ALU.mult))
            for k in range(2):
                last = V.tensor_tensor(oh[:, k], oh[:, k], gw[:, 4 + k, :].unsqueeze(2).broadcast_to(L3), ALU.mult)
            link(last)
            link(V.tensor_tensor(gates[:], oh[:, 0], oh[:, 1], ALU.add))
            for i in range(2):
                hh = h_sb[:, 4 * i:4 * i + 4, 0:E8 * R8].rearrange("p t (e r) -> p t e r", e=E8)
                V.tensor_tensor(hh, hh, gates[:, 4 * i:4 * i + 4, :].unsqueeze(3).broadcast_to([P, 4, E8, R8]),
                                ALU.mult).then_inc(hg_made, 1)
            t_round(5)
            for i in range(2):
                dve.wait_ge(hgt_hi, i + 1)
                lo(hgt_hl[:, LO, i * NB:(i + 1) * NB], ps[5 + i][:], hgt_hl[:, HI, i * NB:(i + 1) * NB]).then_inc(hgt_lo, 1)

            dve.wait_ge(rmsw_in, 16)
            for t in range(TILES + 1):
                u = t - 1
                cur, old = t % 3, u % 3
                if u >= 0:
                    dve.wait_ge(max_made, u + 1)
                    dve.wait_ge(rs_made, u + 1)
                    V.tensor_scalar(qs[:, 3, u:u + 1], qs[:, 1, u:u + 1], qs[:, 2, u:u + 1], 1.0 / QMAX, ALU.mult,
                                    ALU.mult).then_inc(s_step, 1)
                if t < TILES:
                    t_round(14 - TILES + t)
                if u >= 0:
                    dve.wait_ge(s_step, 4 * u + 1)
                    V.tensor_scalar(qs[:, 4, u:u + 1], qs[:, 3, u:u + 1], Q_GUARD, None, ALU.max).then_inc(s_step, 1)
                if t < TILES:
                    dve.wait_ge(cond_ready, t + 1)
                    dve.wait_ge(sq_made, t + 1)
                    if t >= 3:
                        dve.wait_ge(q1_made, t - 2)
                    V.tensor_tensor(cw[:, cur, :], ps[CB[t % 4]][:], rmsw[:], ALU.mult).then_inc(cw_made, 1)
                if u >= 0:
                    dve.wait_ge(s_step, 4 * u + 2)
                    V.reciprocal(qs[:, 5, u:u + 1], qs[:, 4, u:u + 1]).then_inc(s_step, 1)
                if t < TILES:
                    V.tensor_scalar(qs[:, 0, t:t + 1], ssq[:, t:t + 1], 1.0 / H, RMS_EPS, ALU.mult,
                                    ALU.add).then_inc(ms_made, 1)
                    dve.wait_ge(cw_made, t + 1)
                    V.tensor_reduce(qs[:, 1, t:t + 1], cw[:, cur, :], X, ALU.max,
                                    apply_absolute_value=True).then_inc(max_made, 1)
                if u >= 0:
                    dve.wait_ge(s_step, 4 * u + 3)
                    V.tensor_tensor(qs[:, 6, u:u + 1], qs[:, 5, u:u + 1], qs[:, 2, u:u + 1], ALU.mult).then_inc(s_step, 1)
                    dve.wait_ge(s_step, 4 * u + 4)
                    V.tensor_scalar(cw[:, old, :], cw[:, old, :], qs[:, 6, u:u + 1], ROUND, ALU.mult,
                                    ALU.add).then_inc(q1_scaled, 1)
            dve.wait_ge(wsb_in, 48)

            def gu_out(t, slot, c):
                cols = slice(CO[c], CO[c] + CH[c])
                if c == 0 and not (isinstance(t, int) and t < 2):
                    dve.wait_ge(h_scaled, 2 * t - 2)
                dve.wait_ge(gq_ready, 3 * t + c + 1)
                V.scalar_tensor_tensor(g_sb[:, slot, cols], ps[c][:, 0:CH[c]], qs[:, 4, ds(t, 1)], ws_b[:, 0, cols],
                                       ALU.mult, ALU.mult).then_inc(g_made, 1)
                dve.wait_ge(uq_ready, 3 * t + c + 1)
                V.scalar_tensor_tensor(u_sb[:, slot, cols], ps[3 + c][:, 0:CH[c]], qs[:, 4, ds(t, 1)], ws_b[:, 1, cols],
                                       ALU.mult, ALU.mult).then_inc(u_made, 1)

            def h_quant(t, slot):
                dve.wait_ge(h_made, 3 * t + 3)
                c0 = qs[:, 7, 4 * slot:4 * slot + 1]
                s2 = qs[:, 7, 4 * slot + 1:4 * slot + 2]
                i2 = qs[:, 7, 4 * slot + 2:4 * slot + 3]
                V.tensor_reduce(c0, g_sb[:, slot, :], X, ALU.max, apply_absolute_value=True).then_inc(hq, 1)
                dve.wait_ge(hq, 3 * t + 1)
                V.tensor_scalar(s2, c0, 1.0 / QMAX, Q_GUARD, ALU.mult, ALU.max).then_inc(hq, 1)
                dve.wait_ge(hq, 3 * t + 2)
                V.reciprocal(i2, s2).then_inc(hq, 1)
                if not (isinstance(t, int) and t < 1):
                    dve.wait_ge(q2_made, 2 * t)
                dve.wait_ge(hq, 3 * t + 3)
                for cols in Q2_PARTS:
                    V.tensor_scalar(h_rnd[:, cols], g_sb[:, slot, cols], i2, ROUND, ALU.mult, ALU.add).then_inc(h_scaled, 1)

            def o_out(t, slot):
                dve.wait_ge(o_ready, t + 1)
                if not (isinstance(t, int) and t < 2):
                    dve.wait_ge(r_made, t - 1)
                V.scalar_tensor_tensor(o_sb[:, slot, :], ps[7][:], qs[:, 7, 4 * slot + 1:4 * slot + 2], wsd_b[:],
                                       ALU.mult, ALU.mult).then_inc(o_made, 1)

            def l1_step(t, slot):
                gu_out(t, slot, 0)
                gu_out(t, slot, 1)
                h_quant(t - 1, 1 - slot)
                gu_out(t, slot, 2)
                o_out(t - 2, slot)

            for t in range(2):
                for c in range(3):
                    gu_out(t, t, c)
            h_quant(0, 0)
            for t in (2, 3):
                l1_step(t, t % 2)
            with dve.Fori(0, TILES // 2 - 2) as j:
                for d in range(2):
                    l1_step(2 * j + 4 + d, d)
            t, slot = TILES - 1, 1
            c0, s2, i2, c1 = (qs[:, 7, 4 * slot + i:4 * slot + i + 1] for i in range(4))
            dve.wait_ge(h_made, 3 * t + 2)
            V.tensor_reduce(c1, g_sb[:, slot, 0:CO[2]], X, ALU.max, apply_absolute_value=True)
            dve.wait_ge(h_made, 3 * t + 3)
            link(V.tensor_reduce(c0, g_sb[:, slot, CO[2]:F], X, ALU.max, apply_absolute_value=True))
            link(V.tensor_scalar(c1, c1, c0, 1.0 / QMAX, ALU.max, ALU.mult))
            link(V.tensor_scalar(s2, c1, Q_GUARD, None, ALU.max))
            link(V.reciprocal(i2, s2))
            dve.wait_ge(q2_made, 2 * t)
            for cols in Q2_PARTS:
                V.tensor_scalar(h_rnd[:, cols], g_sb[:, slot, cols], i2, ROUND, ALU.mult, ALU.add).then_inc(h_scaled, 1)
            o_out(TILES - 2, 0)
            dve.wait_ge(q2t_ready, 2 * t + 2)
            V.tensor_copy(q2t[:, slot, 6:10, :], psb[0][:, 0:4 * P].rearrange("p (j m) -> p j m", j=4))
            V.tensor_copy(q2t[0:FREM, slot, 10, :], psb[0][0:FREM, 4 * P:5 * P]).then_inc(last_q2t_out, 1)
            dve.wait_ge(r_made, t - 1)
            dve.wait_ge(x1t_out, TILES)
            dve.wait_ge(out_done[slot], 16 * (TILES // 2 - 1))
            for i in range(2):
                cols = slice(i * HH, (i + 1) * HH)
                dve.wait_ge(o_ready, t + i + 1)
                V.scalar_tensor_tensor(o_sb[:, slot, cols], ps[7 if i == 0 else 1][:, 0:HH],
                                       qs[:, 7, 4 * slot + 1:4 * slot + 2], wsd_b[:, cols], ALU.mult, ALU.mult).then_inc(o_made, 1)
                dve.wait_ge(o_made, t + i + 1)
                V.tensor_tensor(r_sb[:, slot, cols], o_sb[:, slot, cols], x1t[:, t, cols], ALU.add).then_inc(last_made, 1)

        @block.tensor
        def _(pe):
            mm, tr = nc.tensor.matmul, nc.tensor.transpose

            def w_eff(c):
                slot = VU_SLOT[c]
                pe.wait_ge(wg_lo, VU_TURN[c])
                for i in range(KT):
                    for w, v in THREE:
                        last = mm(ps[i][:], wg_hl[:, slot, w, i * P:(i + 1) * P], wg_hl[:, slot, v, H:2 * H],
                                  start=(c == 0 and (w, v) == THREE[0]), stop=False)
                last.then_inc(wg_used, 1)

            def delta():
                pe.wait_ge(vr_ready, 2)
                pe.wait_ge(c_ready, 2)
                for i in range(KT):
                    mm(ps[i][:], vr_hl[:, i * P:(i + 1) * P], c_hl[:], start=False, stop=True).then_inc(we_ready, 1)

            def lora_in(n):
                pe.wait_ge(ag_made, KT * (n + 1))
                for i in ((0, 1), (2,))[n]:
                    pe.wait_ge(x_in[i], 16)
                for j in range(KT):
                    for k in range(KT):
                        last = mm(ps[UP[1]][:, j * P:(j + 1) * P], ag[n][:, j, k, :],
                                  x_raw[:, k, n * NB + j * P:n * NB + (j + 1) * P], start=(k == 0), stop=(k == KT - 1))
                last.then_inc(tg_ready, 1)

            def gate_up_base(bank, slot, n, gu, first=False):
                for k in range(KT):
                    if first and k % 2 == 0:
                        pe.wait_ge(x_lo, k // 2 + 1)
                    for w, v in THREE:
                        mm(bank[:], wg_hl[:, slot, w, gu * H + k * P:gu * H + (k + 1) * P], x_hl[n][:, v, k, :],
                           start=(k == 0 and (w, v) == THREE[0]), stop=False)

            def gate_up_lora(bank, slot, n, gu):
                for g in range(2):
                    for w, v in THREE:
                        last = mm(bank[:, g * GT:(g + 1) * GT], b_hl[:, slot, w, g, gu * P:(gu + 1) * P],
                                  tg_hl[:, n, v, gu, g * GT:(g + 1) * GT], start=False,
                                  stop=(g == 1 and (w, v) == THREE[-1]))
                last.then_inc(gate_ready if gu == 0 else wg_used, 1)

            def gate_up(s, slot, n, first=False):
                pe.wait_ge(wg_lo, WCH + s + 1)
                if not (isinstance(s, int) and s < 1):
                    pe.wait_ge(silu_done, s)
                gate_up_base(ps[GATE], slot, n, 0)
                pe.wait_ge(b_lo, s + 1)
                if first:
                    pe.wait_ge(tg_lo, n + 1)
                gate_up_lora(ps[GATE], slot, n, 0)
                if not (isinstance(s, int) and s < 2):
                    pe.wait_ge(act_made, s - 1)
                gate_up_base(ps[UP[slot]], slot, n, 1)
                gate_up_lora(ps[UP[slot]], slot, n, 1)

            def down(s, slot, n, first=False, end=False):
                pe.wait_ge(ad_lo, s + 1)
                pe.wait_ge(wd_lo, s + 1)
                pe.wait_ge(act_lo, s + 1)
                if first:
                    if n:
                        pe.wait_ge(td_masked, n)
                    else:
                        pe.wait_ge(we_lo, KT)
                for g in range(2):
                    for w, v in THREE:
                        mm(ps[TD][:, g * GT:(g + 1) * GT], ad_hl[:, slot, w, g * P:(g + 1) * P],
                           act_hl[:, slot, v, g * GT:(g + 1) * GT], start=(first and g == 0 and (w, v) == THREE[0]),
                           stop=(end and g == 1 and (w, v) == THREE[-1]), skip_group_check=True)
                for m in range(KT):
                    if first and n:
                        pe.wait_ge(y_lo, KT * (n - 1) + m + 1)
                    for w, v in THREE:
                        last = mm(ps[m][:], wd_hl[:, slot, w, m * P:(m + 1) * P], act_hl[:, slot, v, :],
                                  start=(first and (w, v) == THREE[0]), stop=False)
                last.then_inc(down_done, 1)

            def lora_down(n):
                pe.wait_ge(td_lo, n + 1)
                pe.wait_ge(bd_lo, n + 1)
                for m in range(KT):
                    for g in range(2):
                        for w, v in THREE:
                            last = mm(ps[m][:, g * GT:(g + 1) * GT], bd_hl[:, w, g, m * P:(m + 1) * P],
                                      td_hl[:, v, g * GT:(g + 1) * GT], start=False,
                                      stop=(g == 1 and (w, v) == THREE[-1]))
                    last.then_inc(y_ready, 1)

            w_eff(0)
            w_eff(1)
            pe.wait_ge(urs_ready, 1)
            mm(ps[TD][0:4, :], smalls[0:4, s_at["r"]], ur[:], start=True, stop=True).then_inc(cmix_ready, 1)
            pe.wait_ge(wg_lo, STEP0_TURN)
            gate_up_base(ps[GATE], 0, 0, 0, first=True)
            gate_up_base(ps[UP[0]], 0, 0, 1)
            w_eff(2)
            lora_in(0)
            w_eff(3)
            delta()
            pe.wait_ge(b_lo, 1)
            pe.wait_ge(tg_lo, 1)
            gate_up_lora(ps[GATE], 0, 0, 0)
            gate_up_lora(ps[UP[0]], 0, 0, 1)
            gate_up(1, 1, 0)
            down(0, 0, 0, first=True)
            gate_up(2, 0, 0)
            down(1, 1, 0)
            with pe.Fori(0, (FT - 5) // 2) as j:
                gate_up(2 * j + 3, 1, 0)
                down(2 * j + 2, 0, 0)
                gate_up(2 * j + 4, 0, 0)
                down(2 * j + 3, 1, 0)
            gate_up(FT - 2, 1, 0)
            down(FT - 3, 0, 0)
            gate_up(FT - 1, 0, 0)
            pe.wait_ge(act_made, FT - 1)
            lora_in(1)
            down(FT - 2, 1, 0)
            pe.wait_ge(x_lo, 3)
            gate_up(FT, 1, 1, first=True)
            down(FT - 1, 0, 0, end=True)
            gate_up(FT + 1, 0, 1)
            lora_down(0)
            down(FT, 1, 1, first=True)
            gate_up(FT + 2, 1, 1)
            down(FT + 1, 0, 1)
            with pe.Fori(0, (FT - 3) // 2) as j:
                gate_up(2 * j + FT + 3, 0, 1)
                down(2 * j + FT + 2, 1, 1)
                gate_up(2 * j + FT + 4, 1, 1)
                down(2 * j + FT + 3, 0, 1)

            ZB = (5, 6, 7, 5, 5, 0, 1, 2)

            def z(q):
                n, m = divmod(q, KT)
                pe.wait_ge(y_lo, KT * (n + 1))
                if q == 0:
                    pe.wait_ge(silu_done, STEPS)
                    pe.wait_ge(act_made, STEPS)
                if q in (3, 4):
                    pe.wait_ge(x1_made, 1 if q == 3 else 4)
                for k in range(KT):
                    for w, v in THREE:
                        last = mm(ps[ZB[q]][:], we_hl[:, w, k, m * P:(m + 1) * P], y_hl[:, v, k, :],
                                  start=(k == 0 and (w, v) == THREE[0]), stop=(k == KT - 1 and (w, v) == THREE[-1]))
                last.then_inc(z_ready, 1)

            def h_logits(t, bank, at):
                for k in range(KT):
                    last = mm(ps[bank][:, at * HT:(at + 1) * HT], x_raw[:, k, t * P:(t + 1) * P], awr[:, k, :],
                              start=(k == 0), stop=(k == KT - 1))
                last.then_inc(h_ready, 1)

            z(0)
            z(1)
            pe.wait_ge(ws_made, 1)
            pe.wait_ge(const_in, 16)
            tr(ps[7][0:2 * 2 * FT + 8, 0:P], ws_all[:], ident).then_inc(wst_ready, 1)
            down(STEPS - 1, 1, 1, end=True)
            pe.wait_ge(wst_out, 1)
            z(2)
            z(3)
            lora_down(1)
            pe.wait_ge(awr_in, 16)
            pe.wait_ge(x1_made, 4)
            for t in range(3):
                h_logits(t, 4, t)
            for q in range(4, 8):
                z(q)

            def x1_transpose(t):
                if t in (0, 1, 2):
                    pe.wait_ge(x1_made, 5)
                else:
                    pe.wait_ge(x1t_out, t - 2)
                for k in range(KT):
                    last = tr(ps[(5, 6, 7)[t % 3]][:, k * P:(k + 1) * P], x_raw[:, k, t * P:(t + 1) * P], ident)
                last.then_inc(x1t_ready, 1)

            for t in range(4):
                x1_transpose(t)
            pe.wait_ge(x1_made, 8)
            for t in range(3, 6):
                h_logits(t, 3, t - 3)
            pe.wait_ge(h_out, 1)
            for t in range(6, 8):
                h_logits(t, 4, t - 6)

            def cond(t):
                if t == 2:
                    pe.wait_ge(h_out, 2)
                if t >= 4:
                    pe.wait_ge(cw_made, t - 3)
                for k in range(KT):
                    for w, v in THREE:
                        mm(ps[CB[t % 4]][:], x1_hl[:, w, k, t * P:(t + 1) * P], wc_hl[v][:, k, :],
                           start=(k == 0 and (w, v) == THREE[0]), stop=False)

            def cond_lora(t):
                if t in (0, 4):
                    pe.wait_ge(hgt_lo, 1 + t // 4)
                for w, v in THREE:
                    last = mm(ps[CB[t % 4]][:], hgt_hl[:, w, t * P:(t + 1) * P], bc_hl[:, v, :], start=False,
                              stop=((w, v) == THREE[-1]))
                last.then_inc(cond_ready, 1)

            def qt_transpose(t):
                pe.wait_ge(q1_made, t + 1)
                if t == 1:
                    pe.wait_ge(hgt_lo, 2)
                if t >= 2:
                    pe.wait_ge(qt_out, t - 1)
                for k in range(KT):
                    last = tr(psb[(7, 6)[t % 2]][:, k * P:(k + 1) * P], q1[:, t % 4, k * P:(k + 1) * P], identb[:])
                last.then_inc(qt_ready, 1)

            pe.wait_ge(x1_lo, 8)
            pe.wait_ge(wc_lo, 1)
            pe.wait_ge(bc_lo, 1)
            pe.wait_ge(ident_b, 1)
            cond(0)
            for t in range(4, TILES):
                x1_transpose(t)
            cond(1)
            pe.wait_ge(x1t_out, TILES)
            for t in range(TILES):
                pe.wait_ge(hg_made, 1 + t // 4)
                last = tr(ps[5 + t // 4][:, (t % 4) * P:(t % 4 + 1) * P], h_sb[:, t, 0:E8 * R8], ident)
                if t % 4 == 3:
                    last.then_inc(hgt_ready, 1)
            cond(2)
            for t in range(3):
                cond_lora(t)
            for t in range(3, TILES):
                cond(t)
                cond_lora(t)
                if t >= 4:
                    qt_transpose(t - 4)

            def l1_gate_up(t, c):
                for gu, made in ((0, g_made), (1, u_made)):
                    if not (isinstance(t, int) and t < 1):
                        pe.wait_ge(made, 3 * t + c - 2)
                    for k in range(KT):
                        last = mm(ps[3 * gu + c][:, 0:CH[c]], qt[:, t, k, :], wq[:, gu, k, CO[c]:CO[c] + CH[c]],
                                  start=(k == 0), stop=(k == KT - 1))
                    last.then_inc((gq_ready, uq_ready)[gu], 1)

            def q2_transpose(t, slot, part, bank=6, parts_read=None):
                pe.wait_ge(q2_made, 2 * t + part + 1)
                if parts_read is None:
                    parts_read = 2 * t + part
                if not (isinstance(parts_read, int) and parts_read < 1):
                    pe.wait_ge(q2t_out, parts_read)
                blocks = range(6) if part == 0 else range(6, FT)
                for i, j in enumerate(blocks):
                    m = min(P, F - j * P)
                    last = tr(psb[bank][0:m, i * P:(i + 1) * P], q2[:, slot, j * P:j * P + m], identb[:])
                last.then_inc(q2t_ready, 1)

            def l1_down_halves(t, slot):
                pe.wait_ge(o_made, t)
                pe.wait_ge(q2t_out, 2 * t + 1)
                for i in range(2):
                    for j in range(FT):
                        if i == 0 and j == 6:
                            pe.wait_ge(last_q2t_out, 1)
                        m = min(P, F - j * P)
                        last = mm(ps[7 if i == 0 else 1][:, 0:HH], q2t[0:m, slot, j, :], wqd[0:m, j, i * HH:(i + 1) * HH],
                                  start=(j == 0), stop=(j == FT - 1))
                    last.then_inc(o_ready, 1)

            def l1_down(t, slot):
                if not (isinstance(t, int) and t < 1):
                    pe.wait_ge(o_made, t)
                for j in range(FT):
                    if j in (0, 6):
                        pe.wait_ge(q2t_out, 2 * t + (1 if j == 0 else 2))
                    m = min(P, F - j * P)
                    last = mm(ps[7][:], q2t[0:m, slot, j, :], wqd[0:m, j, :], start=(j == 0), stop=(j == FT - 1))
                last.then_inc(o_ready, 1)

            def l1_step(t, slot):
                l1_gate_up(t, 0)
                l1_gate_up(t, 1)
                q2_transpose(t - 2, slot, 0)
                l1_gate_up(t, 2)
                q2_transpose(t - 2, slot, 1)
                l1_down(t - 2, slot)

            pe.wait_ge(t_quant, 8)
            pe.wait_ge(h_out, 3)
            pe.wait_ge(hgt_lo, 1)
            pe.wait_ge(qt_out, 1)
            for c in range(3):
                pe.wait_ge(cw_made, TILES if c == 2 else TILES - 1)
                l1_gate_up(0, c)
                qt_transpose(TILES - 4 + c)
            qt_transpose(TILES - 1)
            for c in range(3):
                l1_gate_up(1, c)
            pe.wait_ge(qt_out, TILES)
            pe.wait_ge(t_quant, 14)
            for c in range(3):
                l1_gate_up(2, c)
            q2_transpose(0, 0, 0)
            q2_transpose(0, 0, 1)
            l1_down(0, 0)
            l1_step(3, 1)
            with pe.Fori(0, TILES // 2 - 2) as j:
                for d in range(2):
                    l1_step(2 * j + 4 + d, d)
            for t in (TILES - 2, TILES - 1):
                first = t == TILES - 2
                q2_transpose(t, t % 2, 0, parts_read=2 * t if first else 2 * t - 1)
                pe.wait_ge(g_made, 3 * TILES)
                q2_transpose(t, t % 2, 1, bank=0, parts_read=0 if first else 2 * t)
                if t < TILES - 1:
                    l1_down(t, t % 2)
                else:
                    l1_down_halves(t, t % 2)


def kernel(**inputs):
    import numpy as np
    import concourse.bacc as bacc
    from concourse.bass_utils import run_bass_kernel_spmd as run

    g = {k: np.asarray(v) for k, v in inputs.items()}

    def pad_f(w, axis):
        z = list(w.shape)
        z[axis] = FP - F
        return np.concatenate([w, np.zeros(z, w.dtype)], axis)

    wg, wu = pad_f(g["L0_cond_W_gate"], 0), pad_f(g["L0_cond_W_up"], 0)
    bg, bu = (pad_f(g[k][0], 1) for k in ("L0_cond_B_gate", "L0_cond_B_up"))
    ag, au = g["L0_cond_A_gate"][0], g["L0_cond_A_up"][0]
    smalls = np.zeros((P, 17), np.float32)
    smalls[:, 0:4] = np.concatenate([g["L0_ffn_S_top"], g["L0_ffn_S_tail"]]).reshape(KT, P).T
    smalls[0:64, 4] = g["L0_ffn_alpha"]
    smalls[0:64, 5] = g["L0_ffn_beta"]
    smalls[0:4, 6] = g["L0_ffn_S_tail_r"]
    smalls[0:4, 7] = g["L0_ffn_D"]
    smalls[:, 8:12] = g["L0_ffn_bias"].reshape(KT, P).T
    smalls[0:4, 12:16] = g["L0_ffn_R"]
    v_all = np.concatenate([g["L0_ffn_Vh_top"], g["L0_ffn_Vh_tail"]], 0).reshape(KT, P, H)
    ut_all = np.concatenate([g["L0_ffn_U_top"], g["L0_ffn_U_tail"]], 1).T.reshape(KT, P, H)
    p = np.arange(P)
    mask_b = (p[:, None] // RANK == np.arange(GT)[None, :] // SEQ)
    mask_q = ((p[:, None] % 64) // RANK == p[None, :] // SEQ)
    smalls[:, 16] = p
    pat = np.broadcast_to((p[:, None] % RANK + 2 * P * np.arange(FT)[None, :])[:, :, None], (P, FT, 4)).reshape(P, 4 * FT)
    iota = np.broadcast_to(np.arange(E8), (P, TILES, E8)).reshape(P, TILES * E8)
    consts = np.concatenate([smalls, pat, LORA_SCALE * np.concatenate([mask_b, mask_q], 1), np.eye(P), iota], 1)
    ids = g["itok_B_2_6"]
    ints = np.concatenate([np.broadcast_to(ids, (P, BATCH)), np.repeat(ids.reshape(4, GB), RANK, axis=1).T,
                           np.repeat(g["itok_B_0_7"].reshape(TILES, P // SEQ), SEQ, axis=1).T], 1)
    vr = np.zeros((4, 32, H), np.float32)
    vr[:, 0:4] = g["L0_ffn_Vh_tail_r"]
    l1g, l1u, l1d = g["L1_ffn_Wg"], g["L1_ffn_Wu"], g["L1_ffn_Wd"]
    arrays = {
        "x_t": g["x"].reshape(T, KT, P).transpose(2, 1, 0),
        "ints": ints.astype(np.int32),
        "consts": consts.astype(np.float32),
        "w_vu": np.concatenate([v_all, ut_all], 2),
        "vr": vr.reshape(P, H),
        "ur": g["L0_ffn_U_tail_r"].T,
        "w_gu": np.stack([wg, wu]).reshape(2, FT, P, KT, P).transpose(1, 4, 0, 3, 2).reshape(FT, P, 2 * H),
        "w_d": pad_f(g["L0_cond_W_down"], 1).T.reshape(FT, P, H),
        "a_gu": np.stack([ag, au]).reshape(2, EXPERTS, RANK, KT, P).transpose(1, 4, 3, 0, 2).reshape(EXPERTS, P, 2 * KT * RANK),
        "a_d": pad_f(g["L0_cond_A_down"][0], 2).reshape(EXPERTS, RANK, FT, P).transpose(0, 3, 2, 1).reshape(EXPERTS, P, FT * RANK),
        "b_gu": np.stack([bg, bu]).reshape(2, EXPERTS, FT, P, RANK).transpose(2, 1, 4, 0, 3).reshape(FT * EXPERTS * RANK, 2 * P),
        "b_d": g["L0_cond_B_down"][0].transpose(0, 2, 1).reshape(EXPERTS * RANK, H),
        "w_nat": np.concatenate([pad_f(l1g, 0).reshape(FT, P, H), pad_f(l1u, 0).reshape(FT, P, H),
                                 pad_f(l1d, 1).reshape(KT, P, FT, P).transpose(2, 1, 0, 3).reshape(FT, P, H)], 2),
        "wg_t": l1g.T.reshape(KT, P, F),
        "wu_t": l1u.T.reshape(KT, P, F),
        "wd_t": pad_f(l1d, 1).T.reshape(FT, P, H).transpose(1, 0, 2),
        "wc_t": g["L1_cond_W"].T.reshape(KT, P, H).transpose(1, 0, 2),
        "awr": np.concatenate([g["L1_cond_A"].reshape(E8 * R8, H), g["L1_cond_Wr"]], 0).T.reshape(KT, P, HT).transpose(1, 0, 2),
        "bc": g["L1_cond_B"].transpose(0, 2, 1).reshape(E8 * R8, H),
        "rmsw": np.broadcast_to(g["L1_ffn_rmsnorm_weight"], (P, H)),
    }
    arrays = {k: np.ascontiguousarray(v) for k, v in arrays.items()}
    nc = bacc.Bacc("TRN2", target_bir_lowering=False, num_devices=1)
    aps = {k: nc.dram_tensor(k + "_dram", v.shape, mybir.dt.from_np(v.dtype), kind="ExternalInput").ap()
           for k, v in arrays.items()}
    scratch = nc.dram_tensor("scale_scratch", [2 * 2 * FT + 8, P], mybir.dt.float32).ap()
    out = nc.dram_tensor("out_dram", [TILES, P, H], mybir.dt.float32, kind="ExternalOutput").ap()
    build(nc, aps, scratch, out)
    r = run(nc, [{k + "_dram": v for k, v in arrays.items()}], core_ids=[0])
    return r.results[0]["out_dram"].reshape(g["x"].shape)
```
